# Optimizing a Trainium2 kernel written in Bass

```python
import numpy as np
import jax
import jax.numpy as jnp

def _softmax(x, axis=-1):
    return jax.nn.softmax(x, axis=axis)

def _gelu(x):
    return jax.nn.gelu(x, approximate=True)

def _silu(x):
    return jax.nn.silu(x)

def _sigmoid(x):
    return jax.nn.sigmoid(x)

def _layernorm(x, axis=-1, eps=1e-05):
    m = jnp.mean(x, axis=axis, keepdims=True)
    v = jnp.var(x, axis=axis, keepdims=True)
    return (x - m) / jnp.sqrt(v + eps)

def _scatter_add(tgt, idx, src, axis=0):
    return tgt.at[idx].add(src)

def _segment_sum(src, seg, n):
    return jax.ops.segment_sum(src, seg, n)
kernel_name = 'mk_sandwich_d1_jaxref_r2_dba93c'

def setup_inputs(seed: int=0):
    np.random.seed(seed)
    _w = jnp.asarray

    def _L0_attn_setup():
        import math
        import jax, jax.numpy as jnp
        import numpy as np
        B, S, D, H = (2, 1024, 512, 16)
        HD = D // H
        key = jax.random.key(seed)
        k1, k2, k3 = jax.random.split(key, 3)
        h = jax.random.normal(k1, (B, S, D), dtype=jnp.float32)
        Wqvk = jax.random.normal(k2, (D, 3 * D), dtype=jnp.float32) * (1.0 / math.sqrt(D))
        Wo = jax.random.normal(k3, (D, D), dtype=jnp.float32) * (1.0 / math.sqrt(D))
        return {'h': h, 'Wqvk': Wqvk, 'Wo': Wo}
    _L0_attn_in = _L0_attn_setup()

    def _L0_ffn_setup():
        import jax, jax.numpy as jnp
        import numpy as np
        B, S, D_MODEL, D_FF = (4, 1024, 512, 2048)

        def _quantum_transform(hidden, theta, w_real, w_imag):
            imag = w_imag * jnp.sin(theta + hidden * 0.1)
            quantum_phase = jnp.cos(theta) * w_real + jnp.sin(theta) * w_imag
            return hidden + quantum_phase * imag * 0.1
        key = jax.random.key(seed)
        ks = jax.random.split(key, 8)
        return {'x': jax.random.normal(ks[0], (B, S, D_MODEL), dtype=jnp.float32), 'W1': jax.random.normal(ks[1], (D_MODEL, D_FF), dtype=jnp.float32) * (1.0 / np.sqrt(D_MODEL)), 'b1': jnp.zeros((D_FF,), dtype=jnp.float32), 'quantum_phases': jax.random.normal(ks[2], (D_FF,), dtype=jnp.float32) * (2.0 * np.pi), 'quantum_weights_real': jax.random.normal(ks[3], (D_FF,), dtype=jnp.float32) * 0.1, 'quantum_weights_imag': jax.random.normal(ks[4], (D_FF,), dtype=jnp.float32) * 0.1, 'W2': jax.random.normal(ks[5], (D_FF, D_MODEL), dtype=jnp.float32) * (1.0 / np.sqrt(D_FF)), 'b2': jnp.zeros((D_MODEL,), dtype=jnp.float32)}
    _L0_ffn_in = _L0_ffn_setup()
    _d = {'L0_attn_h': _L0_attn_in['h'], 'L0_attn_Wqvk': _L0_attn_in['Wqvk'], 'L0_attn_Wo': _L0_attn_in['Wo'], 'L0_ffn_W1': _L0_ffn_in['W1'], 'L0_ffn_b1': _L0_ffn_in['b1'], 'L0_ffn_quantum_phases': _L0_ffn_in['quantum_phases'], 'L0_ffn_quantum_weights_real': _L0_ffn_in['quantum_weights_real'], 'L0_ffn_quantum_weights_imag': _L0_ffn_in['quantum_weights_imag'], 'L0_ffn_W2': _L0_ffn_in['W2'], 'L0_ffn_b2': _L0_ffn_in['b2']}
    _x0 = _d['L0_attn_h']
    _d['L0_attn_h'] = jax.random.normal(jax.random.fold_in(jax.random.key(seed), 1), (8, 1024, 512), dtype=_x0.dtype)
    del _x0
    return _d

def reference(L0_attn_h, L0_attn_Wqvk, L0_attn_Wo, L0_ffn_W1, L0_ffn_b1, L0_ffn_quantum_phases, L0_ffn_quantum_weights_real, L0_ffn_quantum_weights_imag, L0_ffn_W2, L0_ffn_b2):

    def _L0_attn_ref(h, Wqvk, Wo):
        import math
        import jax, jax.numpy as jnp
        import numpy as np
        B, S, D, H = (2, 1024, 512, 16)
        HD = D // H
        b, s, d = h.shape
        qvk = (h @ Wqvk).reshape(b, s, 3, H, HD)
        q, v, k = (qvk[:, :, 0], qvk[:, :, 1], qvk[:, :, 2])
        scores = jnp.einsum('bshi,bthi->bsth', q, k)
        mask = jnp.where(jnp.arange(s)[None, :] > jnp.arange(s)[:, None], jnp.float32(-jnp.inf), jnp.float32(0.0))
        scores = scores + mask[None, :, :, None]
        scores = scores / math.sqrt(d)
        weights = jax.nn.softmax(scores, axis=2)
        wv = jnp.einsum('bsth,bthi->bshi', weights, v).reshape(b, s, d)
        return wv @ Wo

    def _L0_ffn_ref(x, W1, b1, quantum_phases, quantum_weights_real, quantum_weights_imag, W2, b2):
        import jax, jax.numpy as jnp
        import numpy as np
        B, S, D_MODEL, D_FF = (4, 1024, 512, 2048)

        def _quantum_transform(hidden, theta, w_real, w_imag):
            imag = w_imag * jnp.sin(theta + hidden * 0.1)
            quantum_phase = jnp.cos(theta) * w_real + jnp.sin(theta) * w_imag
            return hidden + quantum_phase * imag * 0.1
        hidden = jnp.einsum('bsd,df->bsf', x, W1) + b1
        q = _quantum_transform(hidden, quantum_phases, quantum_weights_real, quantum_weights_imag)
        act = jax.nn.relu(q)
        return jnp.einsum('bsf,fd->bsd', act, W2) + b2
    x = L0_attn_h
    x = x + _layernorm(_L0_attn_ref(_layernorm(x, axis=-1), L0_attn_Wqvk, L0_attn_Wo), axis=-1)
    x = x + _layernorm(_L0_ffn_ref(_layernorm(x, axis=-1), L0_ffn_W1, L0_ffn_b1, L0_ffn_quantum_phases, L0_ffn_quantum_weights_real, L0_ffn_quantum_weights_imag, L0_ffn_W2, L0_ffn_b2), axis=-1)
    return x

_drawn_inputs = setup_inputs


def setup_inputs(seed=0):
    import zlib

    import numpy as np

    out = dict(_drawn_inputs(seed))
    spreads = {'L0_ffn_b1': (0.0, 0.1), 'L0_ffn_b2': (0.0, 0.1)}
    factors = {'L0_ffn_quantum_phases': 8.0,
     'L0_ffn_quantum_weights_real': 39.4,
     'L0_ffn_quantum_weights_imag': 8.0}
    for name, (base, spread) in spreads.items():
        noise = np.random.default_rng([zlib.crc32(name.encode()), seed]).standard_normal(out[name].shape)
        drawn = base * np.exp(spread * noise) if base else spread * noise
        out[name] = jnp.asarray(drawn.astype(out[name].dtype))
    for name, factor in factors.items():
        out[name] = (out[name] * factor).astype(out[name].dtype)
    return out
```

```python
import math
from contextlib import ExitStack

import concourse.bass as bass
from concourse import mybir

F32 = mybir.dt.float32
F32R = mybir.dt.float32r
BF16 = mybir.dt.bfloat16
ALU = mybir.AluOpType
ACT = mybir.ActivationFunctionType
AX_X = mybir.AxisListType.X

P = 128
BATCH, SEQ, D = 8, 1024, 512
HEADS, HD = 16, 32
FF = 2048
CH = 512
TPC = CH // P
KT = D // P
CPB = SEQ // CH
NCH = BATCH * CPB
HPG = P // HD
GROUPS = HEADS // HPG
EPS = 1e-5
START = 1
MASKED = -1e30
PASSES = ((0, 0), (0, 1), (1, 0))


def split_weights(nc, block, name, loads, raw, parts, sem_loaded, sem_hi, sem_lo):

    @block.sync
    def _(sp):
        for n, (src, _at) in enumerate(loads):
            if n >= 2:
                sp.wait_ge(sem_lo, n - 1)
            sp.dma_start(raw[:, n % 2, :], src).then_inc(sem_loaded[n % 2], 16)

    @block.scalar
    def _(act):
        for n, (_src, at) in enumerate(loads):
            act.wait_ge(sem_loaded[n % 2], 16 * (n // 2 + 1))
            act.activation(at(0), raw[:, n % 2, :], ACT.Copy).then_inc(sem_hi, 1)

    @block.vector
    def _(dve):
        for n, (_src, at) in enumerate(loads):
            dve.wait_ge(sem_hi, n + 1)
            dve.tensor_tensor(at(1), raw[:, n % 2, :], at(0).bitcast(F32), ALU.subtract).then_inc(sem_lo, 1)


def identity_matrix(pool, tile, sem):
    pool.memset(tile, 0.0).then_inc(sem, 1)
    pool.wait_ge(sem, 1)
    pool.affine_select(out=tile, in_=tile, compare_op=ALU.not_equal, fill=1.0, base=0,
                       pattern=[[-1, P]], channel_multiplier=1).then_inc(sem, 1)


def qkv_phase(nc, x, w_qvk, qk_parts, v_rows):
    MM = 12
    QK = 8
    BANKS = 6
    STAGE = 4
    SCHED = [("mm", m) for m in range(6)] + [("tr", 0), ("mm", 6), ("tr", 1), ("mm", 7), ("tr", 2), ("mm", 8),
                                             ("tr", 3), ("mm", 9), ("mm", 10), ("mm", 11)]
    ctx = ExitStack()
    with ctx:
        def sb(name, shape, dt=F32):
            return ctx.enter_context(nc.sbuf_tensor(name, shape, dt))

        def sem(name):
            return ctx.enter_context(nc.semaphore("q_" + name))

        w = sb("q_w", [P, 2, KT, 3 * D], F32R)
        raw = sb("q_raw", [P, 2, 3 * D])
        xin = sb("q_x", [P, 2, TPC, D])
        xT = sb("q_xT", [P, 2, 2, KT, CH], F32R)
        stats = sb("q_stats", [P, 2, TPC, 6])
        seen = sb("q_seen", [P, 1])
        mv = sb("q_mv", [P, 2, TPC, 2])
        ve = sb("q_ve", [P, 2, TPC])
        rstd = sb("q_rstd", [P, 2, TPC])
        half = sb("q_half", [P, TPC])
        eps = sb("q_eps", [P, TPC])
        ident = sb("q_ident", [P, P])
        stage = sb("q_stage", [P, STAGE, 2, CH], F32R)
        vstage = sb("q_vstage", [P, TPC, D])
        pt = ctx.enter_context(nc.psum_tensor("q_pt", [P, 2, CH], F32))
        pm = ctx.enter_context(nc.psum_tensor("q_pm", [P, BANKS, CH], F32))

        w_loaded = [sem(f"w_loaded{n}") for n in range(2)]
        w_hi, w_lo = sem("w_hi"), sem("w_lo")
        ident_set, half_set = sem("ident_set"), sem("half_set")
        x_loaded = [sem(f"x_loaded{e}") for e in range(2)]
        stats_done, mv_done, normed = sem("stats_done"), sem("mv_done"), sem("normed")
        ve_done, rstd_done = sem("ve_done"), sem("rstd_done")
        tr_done, tr_hi, tr_lo = sem("tr_done"), sem("tr_hi"), sem("tr_lo")
        mm_done, qk_hi, qk_lo, v_out = sem("mm_done"), sem("qk_hi"), sem("qk_lo"), sem("v_out")
        stored = [sem(f"stored{n}") for n in range(STAGE)]
        v_stored = sem("v_stored")
        x_v = x.rearrange("b (c t p) d -> (b c) p t d", p=P, t=TPC)

        with nc.Block() as wblock:
            split_weights(nc, wblock, "q", [(w_qvk[k * P:(k + 1) * P, :], (lambda part, k=k: w[:, part, k, :]))
                                            for k in range(KT)], raw, w, w_loaded, w_hi, w_lo)

            @wblock.gpsimd
            def _(pool):
                identity_matrix(pool, ident[:, :], ident_set)
                pool.memset(half[:, :], -0.5).then_inc(half_set, 1)
                pool.memset(eps[:, :], EPS).then_inc(half_set, 1)

        with nc.Block() as block:
            @block.sync
            def _(sp):
                def load(n, e):
                    sp.dma_start(xin[:, e], x_v[n]).then_inc(x_loaded[e], 16)

                def store(i, e):
                    n = 2 * i + e
                    for m in range(QK):
                        sp.wait_ge(qk_lo, QK * n + m + 1 + QK)
                        sp.dma_start(qk_parts[i, m].rearrange("l p t -> p l t")[:, :, e * CH:(e + 1) * CH],
                                     stage[:, m % STAGE].bitcast(F32)).then_inc(stored[m % STAGE], 16)
                    sp.wait_ge(v_out, TPC * n + TPC + TPC)
                    sp.dma_start(v_rows[i].rearrange("(c t p) d -> c p t d", p=P, t=TPC)[e],
                                 vstage[:, :, :]).then_inc(v_stored, 16)

                for s in (*stored, v_stored):
                    sp.sem_inc(s, START)
                load(0, 0)
                load(1, 1)
                with sp.Fori(0, BATCH - 1) as i:
                    for e in range(2):
                        sp.wait_ge(tr_done, KT * (2 * i + e) + KT)
                        load(2 * i + e + 2, e)
                        store(i, e)
                for e in range(2):
                    store(BATCH - 1, e)
                for s in stored:
                    sp.wait_ge(s, 16 * (QK // STAGE) * NCH + START)
                sp.wait_ge(v_stored, 16 * NCH + START)

            @block.gpsimd
            def _(pool):
                def rstd_of(n, e):
                    pool.wait_ge(mv_done, n + 1)
                    pool.tensor_tensor(ve[:, e], mv[:, e, :, 1], eps[:, :], ALU.add).then_inc(ve_done, 1)
                    pool.wait_ge(ve_done, n + 1)
                    pool.tensor_tensor(rstd[:, e], ve[:, e], half[:, :], ALU.pow).then_inc(rstd_done, 1)

                with pool.Fori(0, BATCH) as i:
                    for e in range(2):
                        rstd_of(2 * i + e, e)

            @block.vector
            def _(dve):
                dve.sem_inc(qk_lo, QK)

                def ln_stats(n, e, turn):
                    dve.wait_ge(x_loaded[e], 16 * turn)
                    for t in range(TPC):
                        last = dve.bn_stats(stats[:, e, t, :], xin[:, e, t, :])
                    last.then_inc(stats_done, 1)
                    dve.wait_ge(stats_done, n + 1)
                    dve.tensor_copy(seen[:, 0:1], stats[:, e, 0, 0:1])
                    for t in range(TPC):
                        last = dve.bn_aggr(mv[:, e, t, :], stats[:, e, t, :])
                    last.then_inc(mv_done, 1)

                def ln_apply(n, e):
                    dve.wait_ge(rstd_done, n + 1)
                    for t in range(TPC):
                        last = dve.tensor_scalar(xin[:, e, t, :], xin[:, e, t, :], mv[:, e, t, 0:1],
                                                 rstd[:, e, t:t + 1], ALU.subtract, ALU.mult)
                    last.then_inc(normed, 1)

                def transposed_lo(n, e, k):
                    dve.wait_ge(tr_hi, KT * n + k + 1)
                    dve.tensor_tensor(xT[:, e, 1, k, :], pt[:, k % 2, :], xT[:, e, 0, k, :].bitcast(F32),
                                      ALU.subtract).then_inc(tr_lo, 1)

                def chunk(i, e, last):
                    n = 2 * i + e
                    if not last:
                        ln_stats(n + 1, 1 - e, i + 1 + e)
                    for kind, m in SCHED:
                        if kind == "tr":
                            if not last:
                                transposed_lo(n + 1, 1 - e, m)
                        elif m < QK:
                            dve.wait_ge(qk_hi, QK * n + m + 1)
                            dve.tensor_tensor(stage[:, m % STAGE, 1], pm[:, m % BANKS, :],
                                              stage[:, m % STAGE, 0].bitcast(F32), ALU.subtract).then_inc(qk_lo, 1)
                        if kind == "mm" and m == 2 and not last:
                            ln_apply(n + 1, 1 - e)

                ln_stats(0, 0, 1)
                ln_apply(0, 0)
                for k in range(KT):
                    transposed_lo(0, 0, k)
                with dve.Fori(0, BATCH - 1) as i:
                    for e in range(2):
                        chunk(i, e, False)
                for e in range(2):
                    chunk(BATCH - 1, e, e == 1)

            @block.scalar
            def _(act):
                act.sem_inc(v_out, TPC)

                def transposed_hi(n, e, k):
                    act.wait_ge(tr_done, KT * n + k + 1)
                    act.activation(xT[:, e, 0, k, :], pt[:, k % 2, :], ACT.Copy).then_inc(tr_hi, 1)

                def chunk(i, e, last):
                    n = 2 * i + e
                    for kind, m in SCHED:
                        if kind == "tr":
                            if not last:
                                transposed_hi(n + 1, 1 - e, m)
                            continue
                        act.wait_ge(mm_done, MM * n + m + 1)
                        if m < QK:
                            act.wait_ge(stored[m % STAGE], 16 * (2 * n + m // STAGE) + START)
                            act.activation(stage[:, m % STAGE, 0], pm[:, m % BANKS, :], ACT.Copy).then_inc(qk_hi, 1)
                        else:
                            if m == QK:
                                act.wait_ge(v_stored, 16 * n + START)
                            act.activation(vstage[:, m - QK, :], pm[:, m % BANKS, :], ACT.Copy).then_inc(v_out, 1)

                for k in range(KT):
                    transposed_hi(0, 0, k)
                with act.Fori(0, BATCH - 1) as i:
                    for e in range(2):
                        chunk(i, e, False)
                for e in range(2):
                    chunk(BATCH - 1, e, e == 1)

            @block.tensor
            def _(pe):
                def transposes(n, e, k, first=False):
                    if not (first and k < 2):
                        pe.wait_ge(tr_lo, KT * n + k - 1)
                    if k == 0:
                        pe.wait_ge(normed, n + 1)
                    for t in range(TPC):
                        last = pe.transpose(pt[:, k % 2, t * P:(t + 1) * P], xin[:, e, t, k * P:(k + 1) * P], ident[:, :])
                    last.then_inc(tr_done, 1)

                def output(n, e, m):
                    before = m - BANKS
                    if 0 <= before:
                        pe.wait_ge(qk_lo, QK * n + before + 1 + QK)
                    elif before + MM < QK:
                        pe.wait_ge(qk_lo, QK * n + before + MM + 1)
                    else:
                        pe.wait_ge(v_out, TPC * n + before + MM - QK + 1)
                    if m == 0:
                        pe.wait_ge(tr_lo, KT * n + KT)
                    terms = [(k, a, b) for k in range(KT) for a, b in PASSES]
                    for j, (k, a, b) in enumerate(terms):
                        if m < QK:
                            col = m * P if m < GROUPS else 2 * D + (m - GROUPS) * P
                            lhs, rhs = w[:, a, k, col:col + P], xT[:, e, b, k, :]
                        else:
                            lhs, rhs = xT[:, e, b, k, (m - QK) * P:(m - QK + 1) * P], w[:, a, k, D:2 * D]
                        last = pe.matmul(pm[:, m % BANKS, :], lhs, rhs, start=(j == 0), stop=(j == len(terms) - 1))
                    last.then_inc(mm_done, 1)

                def chunk(i, e, last):
                    n = 2 * i + e
                    for kind, m in SCHED:
                        if kind == "mm":
                            output(n, e, m)
                        elif not last:
                            transposes(n + 1, 1 - e, m)

                for k in range(KT):
                    transposes(0, 0, k, first=True)
                with pe.Fori(0, BATCH - 1) as i:
                    for e in range(2):
                        chunk(i, e, False)
                for e in range(2):
                    chunk(BATCH - 1, e, e == 1)


QT = SEQ // P
STEPS = [(c, j) for c in range(CPB) for j in range(TPC * (c + 1))]
NS = len(STEPS)
LAST_OF_C = [max(k for k, (c, _j) in enumerate(STEPS) if c == cc) for cc in range(CPB)]


def score_pieces():
    out = []
    for i in range(QT):
        for half in range(i // TPC + 1):
            n = min((i + 1) * P - half * CH, CH)
            per = CH // n
            out += [(i, half, list(range(h, h + per)), n) for h in range(0, HPG, per)]
    return out


PIECES = score_pieces()
PIECES_AT = [0, 5, 5, 5, 5, 5, 5, 4, 4]
MAX_AT = 8
WO_AT = {7: 0, 8: 1, 9: 2, 10: 3, NS: None}
assert sum(PIECES_AT) == len(PIECES)


def shared_work(last):
    out = []
    for g in range(GROUPS):
        ahead = not (last and g == GROUPS - 1)
        n = 0
        for k in range(NS + 1):
            if ahead and k < len(PIECES_AT):
                out += [(g, k, "piece", m) for m in range(n, n + PIECES_AT[k])]
                n += PIECES_AT[k]
            if ahead and k == MAX_AT:
                out.append((g, k, "max", 0))
            if g == GROUPS - 1 and k in WO_AT:
                tiles = range(TPC, QT) if WO_AT[k] is None else [WO_AT[k]]
                out += [(g, k, "wo", t) for t in tiles]
    return out


def attention_phase(nc, x, w_o, qk_parts, v_rows, x1):
    SCALE = 1.0 / math.sqrt(D)
    UNITS = GROUPS
    KQ = 3 * HD
    KM = KQ + 2
    AHEAD = [(0, 0, "piece", m) for m in range(len(PIECES))] + [(0, 0, "max", 0)]
    NAHEAD = len(AHEAD)
    WORK = shared_work(False)
    NWO = QT
    NRED = len(WORK) - NWO
    assert len(WORK) % 2 == 0
    PAIRS = HPG // 2
    NE = NS * PAIRS
    PRING = 2 * PAIRS
    PV_CREDIT, EXP_CREDIT = 2, 2

    ctx = ExitStack()
    with ctx:
        def sb(name, shape, dt=F32):
            return ctx.enter_context(nc.sbuf_tensor("a_" + name, shape, dt))

        def ps(name, shape):
            return ctx.enter_context(nc.psum_tensor("a_" + name, shape, F32))

        def sem(name):
            return ctx.enter_context(nc.semaphore("a_" + name))

        wo = sb("wo", [P, 2, KT, D], F32R)
        qp = [sb(f"qp{b}", [KM, HPG, SEQ], F32R) for b in range(2)]
        kp = [sb(f"kp{b}", [KM, HPG, SEQ], F32R) for b in range(2)]
        vt = sb("vt", [P, 2, QT, P])
        prob = sb("prob", [P, PRING, 2, CH])
        ones = sb("ones", [P, HD])
        ident = sb("ident", [P, P])
        identb, mask_q, mask_k = (sb(n, [P, P], BF16) for n in ("identb", "mask_q", "mask_k"))
        mx = sb("mx", [P, HPG, QT])
        mx2 = sb("mx2", [P, HPG, QT - TPC])
        nm = sb("nm", [HPG * QT, 2, P], F32R)
        rden = sb("rden", [P, CH])
        o = sb("o", [P, CPB, CH])
        oT = sb("oT", [P, 2, GROUPS, SEQ], F32R)
        stats = sb("stats", [P, 2, 6])
        seen = sb("seen", [P, 1])
        mv = sb("mv", [P, 2, 2])
        small = sb("small", [P, 2, 4])
        half = sb("half", [P, 1])
        eps = sb("eps", [P, 1])
        minus = sb("minus", [P, 1])
        y = sb("y", [P, 2, D])
        xr = sb("xr", [P, 2, D])
        pw = ps("pw", [P, 2, CH])
        pst = ps("pst", [P, 2, PAIRS, CH])
        acc = ps("acc", [P, CH])
        den = ps("den", [P, CH])

        w_loaded = [sem(f"w_loaded{n}") for n in range(2)]
        w_hi, w_lo = sem("w_hi"), sem("w_lo")
        const = sem("const")
        qk_loaded = [[sem(f"qk_loaded{b}{c}") for c in range(CPB)] for b in range(2)]
        v_loaded = [sem(f"v_loaded{b}") for b in range(2)]
        work_done, reduced, wo_read = sem("work_done"), sem("reduced"), sem("wo_read")
        max_ready, nm_hi, nm_stored = sem("max_ready"), sem("nm_hi"), sem("nm_stored")
        st_done, exp_done, pv_done = sem("st_done"), sem("exp_done"), sem("pv_done")
        rden_done, acc_read, o_hi, o_lo = sem("rden_done"), sem("acc_read"), sem("o_hi"), sem("o_lo")
        stats_done, mv_done, small_done = sem("stats_done"), sem("mv_done"), sem("small_done")
        xr_loaded = [sem(f"xr_loaded{b}") for b in range(2)]
        y_done = sem("y_done")
        y_stored = [sem(f"y_stored{b}") for b in range(2)]

        with nc.Block() as wblock:
            split_weights(nc, wblock, "a", [(w_o[k * P:(k + 1) * P, :], (lambda part, k=k: wo[:, part, k, :]))
                                            for k in range(KT)], prob[:, 0], wo, w_loaded, w_hi, w_lo)

            @wblock.gpsimd
            def _(pool):
                identity_matrix(pool, ident[:, :], const)
                pool.memset(identb[:, :], 0.0).then_inc(const, 1)
                pool.memset(mask_q[:, :], 0.0).then_inc(const, 1)
                pool.memset(mask_k[:, :], 0.0).then_inc(const, 1)
                pool.wait_ge(const, 5)
                pool.affine_select(out=identb[:, :], in_=identb[:, :], compare_op=ALU.not_equal, fill=1.0, base=0,
                                   pattern=[[-1, P]], channel_multiplier=1)
                pool.affine_select(out=mask_q[:, :], in_=mask_q[:, :], compare_op=ALU.is_ge, fill=MASKED, base=0,
                                   pattern=[[-1, P]], channel_multiplier=1)
                pool.affine_select(out=mask_k[:, :], in_=mask_k[:, :], compare_op=ALU.is_ge, fill=MASKED, base=0,
                                   pattern=[[1, P]], channel_multiplier=-1)
                pool.memset(half[:, :], -0.5)
                pool.memset(eps[:, :], EPS)
                pool.memset(minus[:, :], -1.0)
                pool.memset(ones[:, :], 1.0).then_inc(const, 1)
                for b in range(2):
                    pool.wait_ge(const, 6 + b)
                    pool.memset(kp[b][KQ:KM, :, :].bitcast(F32), 1.0).then_inc(const, 1)

        with nc.Block() as block:
            def red_count(i, items, at):
                return NAHEAD + NRED * i + sum(what != "wo" for _g, _k, what, _n in items[:at + 1])

            @block.sync
            def _(sp):
                x_v = x.rearrange("b (t p) d -> b t p d", p=P)
                x1_v = x1.rearrange("b (t p) d -> b t p d", p=P)

                def load_qk(i, g, b, c, q):
                    m = g if q else GROUPS + g
                    for term, part in enumerate((0, 1, 0) if q else (0, 0, 1)):
                        sp.dma_start((qp if q else kp)[b][term * HD:(term + 1) * HD, :, c * CH:(c + 1) * CH].bitcast(F32),
                                     qk_parts[i, m, part].rearrange("(h r) t -> r h t", r=HD)[:, :, c * CH:(c + 1) * CH]
                                     ).then_inc(qk_loaded[b][c], 16)

                def load_v(i, g, b):
                    sp.dma_start(vt[:, b], v_rows[i].rearrange("(j p) f -> p j f", p=P)[:, :, g * P:(g + 1) * P]
                                 ).then_inc(v_loaded[b], 16)

                def store_max(b):
                    for part in range(2):
                        sp.dma_start(qp[b][KQ + part:KQ + part + 1, :, :].bitcast(F32), nm[:, part, :].bitcast(F32)
                                     ).then_inc(nm_stored, 16)

                def load_x(i, t):
                    sp.dma_start(xr[:, t % 2, :], x_v[i, t]).then_inc(xr_loaded[t % 2], 16)

                def store_tile(i, t, last):
                    sp.wait_ge(y_done, NWO * i + t + 1)
                    sp.dma_start(x1_v[i + 1, t], y[:, t % 2, :]).then_inc(y_stored[t % 2], 16)
                    if t + 2 < QT:
                        load_x(i, t + 2)
                    elif not last:
                        load_x(i + 1, t + 2 - QT)

                def batch(i, last):
                    items = shared_work(last)
                    for g in range(UNITS):
                        b = g % 2
                        more = not (last and g >= UNITS - 2)
                        i2, g2 = (i, g + 2) if g < UNITS - 2 else (i + 1, g - (UNITS - 2))
                        if more:
                            sp.wait_ge(st_done, NE * (UNITS * i + g) + PAIRS * (LAST_OF_C[0] + 1))
                            load_qk(i2, g2, b, 0, True)
                        if g == GROUPS - 1:
                            store_tile(i, 0, last)
                        at = [n for n, it in enumerate(items) if it[0] == g and it[2] == "max"]
                        if at:
                            sp.wait_ge(reduced, red_count(i, items, at[0]))
                            store_max(1 - b)
                        if g == GROUPS - 1:
                            for t in range(1, TPC):
                                store_tile(i, t, last)
                        if more:
                            sp.wait_ge(st_done, NE * (UNITS * i + g) + NE)
                            load_qk(i2, g2, b, 0, False)
                            load_qk(i2, g2, b, 1, True)
                            load_qk(i2, g2, b, 1, False)
                            sp.wait_ge(pv_done, NS * (UNITS * i + g) + NS + PV_CREDIT)
                            load_v(i2, g2, b)
                        if g == GROUPS - 1:
                            for t in range(TPC, QT):
                                store_tile(i, t, last)

                for g in range(2):
                    for c in range(CPB):
                        load_qk(0, g, g, c, True)
                        load_qk(0, g, g, c, False)
                    load_v(0, g, g)
                sp.wait_ge(reduced, NAHEAD)
                store_max(0)
                for s in y_stored:
                    sp.sem_inc(s, START)
                load_x(0, 0)
                load_x(0, 1)
                with sp.Fori(0, BATCH - 1) as i:
                    batch(i, False)
                batch(BATCH - 1, True)
                for s in y_stored:
                    sp.wait_ge(s, 16 * BATCH * QT // 2 + START)

            @block.tensor
            def _(pe):
                def piece(unit, b, at_bank, m):
                    i, half_, heads, n = PIECES[m]
                    diagonal = half_ == i // TPC
                    for s, h in enumerate(heads):
                        last = pe.matmul(pw[:, at_bank, s * n:(s + 1) * n], qp[b][0:KQ, h, i * P:(i + 1) * P],
                                         kp[b][0:KQ, h, half_ * CH:half_ * CH + n], start=True, stop=not diagonal)
                        if diagonal:
                            last = pe.matmul(pw[:, at_bank, (s + 1) * n - P:(s + 1) * n], identb[:, :], mask_q[:, :],
                                             start=False, stop=True)
                    return last

                def shared(i, item, at, unit, b):
                    _g, _k, what, m = item
                    bank = (NAHEAD + at) % 2
                    if what == "piece":
                        if m in (0, FIRST_OF_SECOND):
                            c = int(m > 0)
                            pe.wait_ge(qk_loaded[b][c], 96 * unit)
                        last = piece(unit, b, bank, m)
                    elif what == "max":
                        last = pe.transpose(pw[0:HPG * QT, bank, 0:P], mx[:, :, :].rearrange("p h i -> p (h i)"),
                                            ident[:, :])
                    else:
                        terms = [(g, a, w) for g in range(GROUPS) for w, a in PASSES]
                        for j, (g, a, w) in enumerate(terms):
                            last = pe.matmul(pw[:, bank, :], oT[:, a, g, m * P:(m + 1) * P], wo[:, w, g, :],
                                             start=(j == 0), stop=(j == len(terms) - 1))
                    last.then_inc(work_done, 1)

                def scores(i, g, k, b):
                    c, j = STEPS[k]
                    off = P * max(0, j - TPC * c)
                    n0 = NE * (UNITS * i + g)
                    if k == 0:
                        pe.wait_ge(nm_stored, 32 * (UNITS * i + g) + 32)
                    for pr in range(PAIRS):
                        slot = (PAIRS * k + pr) % 2
                        pe.wait_ge(exp_done, n0 + PAIRS * k + pr - 1 + EXP_CREDIT)
                        for hh in range(2):
                            h = 2 * pr + hh
                            diagonal = j >= TPC * c
                            last = pe.matmul(pst[:, slot, hh, off:CH], kp[b][:, h, j * P:(j + 1) * P],
                                             qp[b][:, h, c * CH + off:(c + 1) * CH], start=True, stop=not diagonal)
                            if diagonal:
                                last = pe.matmul(pst[:, slot, hh, off:off + P], identb[:, :], mask_k[:, :],
                                                 start=False, stop=True)
                        last.then_inc(st_done, 1)

                def weigh(i, g, k, b):
                    c, j = STEPS[k]
                    off = P * max(0, j - TPC * c)
                    pe.wait_ge(exp_done, NE * (UNITS * i + g) + PAIRS * (k + 1) + EXP_CREDIT)
                    if k == 0:
                        pe.wait_ge(v_loaded[b], 16 * (2 * i + g // 2 + 1))
                    if j == 0:
                        pe.wait_ge(acc_read, CPB * (UNITS * i + g) + c + START)
                    for out, wts in ((acc, None), (den, ones)):
                        for h in range(HPG):
                            lhs = vt[:, b, j, h * HD:(h + 1) * HD] if wts is None else wts[:, :]
                            last = pe.matmul(out[h * HD:(h + 1) * HD, off:CH], lhs,
                                             prob[:, (PAIRS * k + h // 2) % PRING, h % 2, off:CH],
                                             start=(j == 0), stop=(k == LAST_OF_C[c]))
                    last.then_inc(pv_done, 1)

                def batch(i, last):
                    items = shared_work(last)
                    at = 0
                    for g in range(UNITS):
                        for k in range(NS + 1):
                            if k < NS:
                                scores(i, g, k, g % 2)
                            if k == NS:
                                weigh(i, g, k - 1, g % 2)
                            while at < len(items) and items[at][0:2] == (g, k):
                                item = items[at]
                                if at < 2:
                                    pe.wait_ge(reduced, NAHEAD + NRED * i)
                                    pe.wait_ge(wo_read, NWO * i + START)
                                elif items[at - 2][2] == "wo":
                                    pe.wait_ge(wo_read, NWO * i + items[at - 2][3] + 1 + START)
                                else:
                                    pe.wait_ge(reduced, red_count(i, items, at - 2))
                                if item[2] == "max":
                                    pe.wait_ge(max_ready, UNITS * i + g + 2)
                                if item[2] == "wo" and item[3] % TPC == 0:
                                    pe.wait_ge(o_lo, CPB * (UNITS * i + g) + item[3] // TPC + 1)
                                shared(i, item, at, 2 * i + (g + 1) // 2 + 1, (g + 1) % 2)
                                at += 1
                            if 0 < k < NS:
                                weigh(i, g, k - 1, g % 2)

                for at, item in enumerate(AHEAD):
                    if at >= 2:
                        pe.wait_ge(reduced, at - 1)
                    if item[2] == "max":
                        pe.wait_ge(max_ready, 1)
                    shared(0, item, at - NAHEAD, 1, 0)
                with pe.Fori(0, BATCH - 1) as i:
                    batch(i, False)
                batch(BATCH - 1, True)

            @block.scalar
            def _(act):
                act.sem_inc(exp_done, EXP_CREDIT)
                act.sem_inc(wo_read, START)

                def exponentials(i, g, k):
                    c, j = STEPS[k]
                    off = P * max(0, j - TPC * c)
                    act.wait_ge(pv_done, NS * (UNITS * i + g) + k - 1 + PV_CREDIT)
                    for pr in range(PAIRS):
                        n = PAIRS * k + pr
                        act.wait_ge(st_done, NE * (UNITS * i + g) + n + 1)
                        act.activation(prob[:, n % PRING, :, off:CH], pst[:, n % 2, :, off:CH], ACT.Exp,
                                       scale=SCALE).then_inc(exp_done, 1)

                def output_hi(i, g, c):
                    m = CPB * (UNITS * i + g) + c
                    act.wait_ge(acc_read, m + 1 + START)
                    act.wait_ge(work_done, NAHEAD + len(WORK) * i)
                    act.activation(oT[:, 0, g, c * CH:(c + 1) * CH], o[:, c, :], ACT.Copy).then_inc(o_hi, 1)

                def wo_norm(i, t, at):
                    s = t % 2
                    act.wait_ge(small_done, 4 * (NWO * i + t) + 4)
                    act.wait_ge(y_stored[s], 16 * (NWO // 2 * i + t // 2) + START)
                    act.activation(y[:, s, :], pw[:, (NAHEAD + at) % 2, :], ACT.Identity, bias=small[:, s, 3:4],
                                   scale=small[:, s, 1:2]).then_inc(wo_read, 1)

                def batch(i, last):
                    items = shared_work(last)
                    for g in range(UNITS):
                        for k in range(NS + 1):
                            if k < NS:
                                exponentials(i, g, k)
                            if k == LAST_OF_C[0] + 2:
                                output_hi(i, g, 0)
                            if k == NS:
                                output_hi(i, g, 1)
                            for at, (gg, kk, what, t) in enumerate(items):
                                if (gg, kk, what) == (g, k, "wo"):
                                    wo_norm(i, t, at)

                with act.Fori(0, BATCH - 1) as i:
                    batch(i, False)
                batch(BATCH - 1, True)

            @block.vector
            def _(dve):
                dve.sem_inc(pv_done, PV_CREDIT)
                dve.sem_inc(acc_read, START)

                def reduce_item(i, items, at, unit):
                    _g, _k, what, m = items[at]
                    base = NAHEAD if items is not AHEAD else 0
                    bank = (base + at) % 2
                    dve.wait_ge(work_done, (NAHEAD + len(WORK) * i if base else 0) + at + 1)
                    done = red_count(i, items, at) if base else at + 1
                    if what == "piece":
                        qt, half_, heads, n = PIECES[m]
                        out = mx2[:, heads[0]:heads[-1] + 1, qt - TPC] if half_ else mx[:, heads[0]:heads[-1] + 1, qt]
                        src = pw[:, bank, 0:n * len(heads)].rearrange("p (h n) -> p h n", n=n)
                        dve.tensor_reduce(out, src, AX_X, ALU.max).then_inc(reduced, 1)
                        if m == len(PIECES) - 1:
                            dve.wait_ge(reduced, done)
                            dve.tensor_tensor(mx[:, :, TPC:QT], mx[:, :, TPC:QT], mx2[:, :, :], ALU.max
                                              ).then_inc(max_ready, 1)
                    else:
                        dve.wait_ge(nm_stored, 32 * unit)
                        src = pw[0:HPG * QT, bank, 0:P]
                        dve.tensor_scalar(nm[:, 0, :], src, -1.0, None, ALU.mult).then_inc(nm_hi, 1)
                        dve.wait_ge(nm_hi, unit + 1)
                        dve.scalar_tensor_tensor(nm[:, 1, :], src, -1.0, nm[:, 0, :].bitcast(F32), ALU.mult,
                                                 ALU.subtract).then_inc(reduced, 1)

                def normalise(i, g, c):
                    m = CPB * (UNITS * i + g) + c
                    dve.wait_ge(pv_done, NS * (UNITS * i + g) + LAST_OF_C[c] + 1 + PV_CREDIT)
                    dve.reciprocal(rden[:, :], den[:, :]).then_inc(rden_done, 1)
                    dve.wait_ge(rden_done, m + 1)
                    dve.tensor_tensor(o[:, c, :], acc[:, :], rden[:, :], ALU.mult).then_inc(acc_read, 1)

                def output_lo(i, g, c):
                    dve.wait_ge(o_hi, CPB * (UNITS * i + g) + c + 1)
                    dve.tensor_tensor(oT[:, 1, g, c * CH:(c + 1) * CH], o[:, c, :],
                                      oT[:, 0, g, c * CH:(c + 1) * CH].bitcast(F32), ALU.subtract).then_inc(o_lo, 1)

                def wo_stats(i, t, at):
                    s = t % 2
                    n = NWO * i + t
                    dve.wait_ge(work_done, NAHEAD + len(WORK) * i + at + 1)
                    dve.bn_stats(stats[:, s, :], pw[:, (NAHEAD + at) % 2, :]).then_inc(stats_done, 1)
                    dve.wait_ge(wo_read, n + START)
                    dve.wait_ge(stats_done, n + 1)
                    dve.tensor_copy(seen[:, :], stats[:, s, 0:1])
                    dve.bn_aggr(mv[:, s, :], stats[:, s, :]).then_inc(mv_done, 1)

                def batch(i, last):
                    items = shared_work(last)
                    for g in range(UNITS):
                        for k in range(NS + 1):
                            if k == NS:
                                normalise(i, g, 1)
                                output_lo(i, g, 1)
                            for at, (gg, kk, what, t) in enumerate(items):
                                if (gg, kk) == (g, k):
                                    if what == "wo":
                                        wo_stats(i, t, at)
                                    else:
                                        reduce_item(i, items, at, UNITS * i + g + 1)
                            if k == LAST_OF_C[0] + 1:
                                normalise(i, g, 0)
                            if k == LAST_OF_C[0] + 2:
                                output_lo(i, g, 0)

                for at in range(NAHEAD):
                    reduce_item(0, AHEAD, at, 0)
                with dve.Fori(0, BATCH - 1) as i:
                    batch(i, False)
                batch(BATCH - 1, True)

            @block.gpsimd
            def _(pool):
                def wo_tile(i, t):
                    n, s = NWO * i + t, t % 2
                    pool.wait_ge(mv_done, n + 1)
                    c = 4 * n
                    pool.tensor_tensor(small[:, s, 0:1], mv[:, s, 1:2], eps[:, :], ALU.add).then_inc(small_done, 1)
                    pool.wait_ge(small_done, c + 1)
                    pool.tensor_tensor(small[:, s, 1:2], small[:, s, 0:1], half[:, :], ALU.pow).then_inc(small_done, 1)
                    pool.wait_ge(small_done, c + 2)
                    pool.tensor_tensor(small[:, s, 2:3], mv[:, s, 0:1], small[:, s, 1:2], ALU.mult
                                       ).then_inc(small_done, 1)
                    pool.wait_ge(small_done, c + 3)
                    pool.tensor_tensor(small[:, s, 3:4], small[:, s, 2:3], minus[:, :], ALU.mult
                                       ).then_inc(small_done, 1)
                    pool.wait_ge(wo_read, n + 1 + START)
                    pool.wait_ge(xr_loaded[s], 16 * (NWO // 2 * i + t // 2 + 1))
                    pool.tensor_tensor(y[:, s, :], y[:, s, :], xr[:, s, :], ALU.add).then_inc(y_done, 1)

                with pool.Fori(0, BATCH - 1) as i:
                    for t in range(QT):
                        wo_tile(i, t)
                for t in range(QT):
                    wo_tile(BATCH - 1, t)


FIRST_OF_SECOND = next(m for m, (i, _half, _heads, _n) in enumerate(PIECES) if i >= TPC)


def ffn_phase(nc, x1, w1, b1, phases, w_real, w_imag, w2, b2, out):
    TWO_PI = 2 * math.pi
    TURN = 6.283185
    PI_IN = 3.1415925
    SLOPE = 0.1
    ROUND = 1.5 * 2 ** 23
    C1 = 201 / 32
    C2 = round((TWO_PI - C1) * 2 ** 20) / 2 ** 20
    C3 = TWO_PI - C1 - C2
    NF = FF // P
    HB = 3
    AR = 2
    STATS_AT, APPLY_AT = 6, 8
    TR_AT = {10: 0, 11: 1, 12: 2, 13: 3}
    POST_AT = (2, 4)

    ctx = ExitStack()
    with ctx:
        def sb(name, shape, dt=F32):
            return ctx.enter_context(nc.sbuf_tensor("f_" + name, shape, dt))

        def sem(name):
            return ctx.enter_context(nc.semaphore("f_" + name))

        w1s = sb("w1", [P, 2, KT, FF], F32R)
        w2s = sb("w2", [P, 2, NF, D], F32R)
        xT = sb("xT", [P, 2, 2, KT, CH], F32R)
        xin = sb("x", [P, 2, TPC, D])
        work = sb("work", [P, TPC, D])
        act_r = sb("act", [P, AR, 2, CH], F32R)
        arg = sb("arg", [P, 2, CH])
        whole = sb("whole", [P, 2, CH])
        b2s = sb("b2", [P, D])
        ident = sb("ident", [P, P])
        vec_rows = sb("vec_rows", [4 * NF, P])
        vec = sb("vec", [P, 4, NF])
        tmp = sb("tmp", [P, 12, NF])
        coef = sb("coef", [P, NF])
        turn0 = sb("turn0", [P, NF])
        stats = sb("stats", [P, 2, TPC, 6])
        seen = sb("seen", [P, 1])
        mv = sb("mv", [P, 2, TPC, 2])
        ve = sb("ve", [P, 2, TPC])
        rstd = sb("rstd", [P, 2, TPC])
        half = sb("half", [P, TPC])
        eps = sb("eps", [P, TPC])
        ph = ctx.enter_context(nc.psum_tensor("f_ph", [P, HB, CH], F32))
        pt = ctx.enter_context(nc.psum_tensor("f_pt", [P, CH], F32))
        py = ctx.enter_context(nc.psum_tensor("f_py", [P, TPC, D], F32))

        w_loaded = [sem(f"w_loaded{n}") for n in range(2)]
        w_hi, w_lo = sem("w_hi"), sem("w_lo")
        const, vec_loaded, b2_loaded = sem("const"), sem("vec_loaded"), sem("b2_loaded")
        vec_turned, vec_step, trig = sem("vec_turned"), sem("vec_step"), sem("trig")
        x_loaded = [sem(f"x_loaded{e}") for e in range(2)]
        stats_done, mv_done, ve_done, rstd_done = sem("stats_done"), sem("mv_done"), sem("ve_done"), sem("rstd_done")
        normed, tr_done, tr_hi, tr_lo = sem("normed"), sem("tr_done"), sem("tr_hi"), sem("tr_lo")
        h_done, arg_done, whole_done, frac_done = sem("h_done"), sem("arg_done"), sem("whole_done"), sem("frac_done")
        sin_done, q_done, relu_done, act_hi, act_lo = (sem(n) for n in ("sin_done", "q_done", "relu_done", "act_hi",
                                                                        "act_lo"))
        w2_used, w2_done, y_read, y_normed, y_final, y_stored = (sem(n) for n in ("w2_used", "w2_done", "y_read", "y_normed", "y_final",
                                                                         "y_stored"))
        x1_v = x1[1:BATCH + 1].rearrange("b (c t p) d -> (b c) p t d", p=P, t=TPC)
        out_v = out.rearrange("b (c t p) d -> (b c) p t d", p=P, t=TPC)
        raw = xin[:, :, :, :].rearrange("p e t d -> p e (t d)")
        b2_rows = b2.rearrange("(o d) -> o d", o=1).broadcast_to([P, D])

        with nc.Block() as wblock:
            pieces = [(w1[k * P:(k + 1) * P, :], (lambda part, k=k: w1s[:, part, k, :])) for k in range(KT)]
            pieces += [(w2.rearrange("(g k p) d -> g p k d", k=4, p=P)[g],
                        (lambda part, g=g: w2s[:, part, 4 * g:4 * g + 4, :].rearrange("p k d -> p (k d)")))
                       for g in range(NF // 4)]
            split_weights(nc, wblock, "f", pieces, raw, None, w_loaded, w_hi, w_lo)

            @wblock.gpsimd
            def _(pool):
                identity_matrix(pool, ident[:, :], const)
                pool.memset(half[:, :], -0.5)
                pool.memset(eps[:, :], EPS)
                for n, v in enumerate((b1, phases, w_real, w_imag)):
                    pool.dma_start(vec_rows[n * NF:(n + 1) * NF, :], v.rearrange("(f p) -> f p", p=P)
                                   ).then_inc(vec_loaded, 16)
                pool.dma_start(b2s[:, :], b2_rows).then_inc(b2_loaded, 16)
                pool.wait_ge(vec_loaded, 64)
                pool.wait_ge(b2_loaded, 16)

        with nc.Block() as vblock:
            @vblock.tensor
            def _(pe):
                pe.transpose(pt[:, 0:4 * NF], vec_rows[:, :], ident[0:4 * NF, 0:4 * NF]).then_inc(vec_turned, 1)

            @vblock.vector
            def _(dve):
                steps = [0]

                def then(ins):
                    steps[0] += 1
                    ins.then_inc(vec_step, 1)
                    dve.wait_ge(vec_step, steps[0])

                bias, th, wr, wi = (vec[:, n, :] for n in range(4))
                turns, thr, sin_a, cos_a, over, sin_t, cos_t = (tmp[:, n, :] for n in range(7))
                dve.wait_ge(vec_turned, 1)
                then(dve.tensor_copy(vec[:, :, :].rearrange("p v f -> p (v f)"), pt[:, 0:4 * NF]))
                then(dve.tensor_scalar(turns, th, 1 / TWO_PI, ROUND, ALU.mult, ALU.add))
                then(dve.tensor_scalar(turns, turns, -ROUND, None, ALU.add))
                then(dve.scalar_tensor_tensor(thr, turns, -C1, th, ALU.mult, ALU.add))
                then(dve.scalar_tensor_tensor(thr, turns, -C2, thr, ALU.mult, ALU.add))
                then(dve.scalar_tensor_tensor(thr, turns, -C3, thr, ALU.mult, ALU.add))
                then(dve.tensor_scalar(sin_a, thr, PI_IN, -PI_IN, ALU.min, ALU.max))
                then(dve.tensor_scalar(cos_a, thr, math.pi / 2, None, ALU.add))
                then(dve.tensor_scalar(over, cos_a, PI_IN, -TWO_PI, ALU.is_gt, ALU.mult))
                then(dve.tensor_tensor(cos_a, cos_a, over, ALU.add))
                then(dve.tensor_scalar(cos_a, cos_a, PI_IN, -PI_IN, ALU.min, ALU.max))
                then(dve.scalar_tensor_tensor(turn0[:, :], bias, SLOPE, thr, ALU.mult, ALU.add))
                then(dve.tensor_scalar(turn0[:, :], turn0[:, :], 1 / TWO_PI, None, ALU.mult))
                dve.wait_ge(trig, 2)
                then(dve.tensor_tensor(cos_t, cos_t, wr, ALU.mult))
                then(dve.tensor_tensor(sin_t, sin_t, wi, ALU.mult))
                then(dve.tensor_tensor(cos_t, cos_t, sin_t, ALU.add))
                then(dve.tensor_tensor(cos_t, cos_t, wi, ALU.mult))
                then(dve.tensor_scalar(coef[:, :], cos_t, SLOPE, None, ALU.mult))

            @vblock.scalar
            def _(act):
                act.wait_ge(vec_step, 11)
                act.activation(tmp[:, 5, :], tmp[:, 2, :], ACT.Sin).then_inc(trig, 1)
                act.activation(tmp[:, 6, :], tmp[:, 3, :], ACT.Sin).then_inc(trig, 1)

        with nc.Block() as block:
            @block.sync
            def _(sp):
                def load(n, e):
                    sp.dma_start(xin[:, e], x1_v[n]).then_inc(x_loaded[e], 16)

                def finish(n):
                    sp.wait_ge(y_final, n + 1)
                    sp.dma_start(out_v[n], work[:, :, :]).then_inc(y_stored, 16)

                sp.sem_inc(y_stored, START)
                load(0, 0)
                load(1, 1)
                with sp.Fori(0, BATCH - 1) as i:
                    for e in range(2):
                        finish(2 * i + e)
                        load(2 * i + e + 2, e)
                for e in range(2):
                    finish(2 * (BATCH - 1) + e)
                sp.wait_ge(y_stored, 16 * NCH + START)

            @block.gpsimd
            def _(pool):
                def rstd_of(number, which):
                    pool.wait_ge(mv_done, number + 1)
                    pool.tensor_tensor(ve[:, which], mv[:, which, :, 1], eps[:, :], ALU.add).then_inc(ve_done, 1)
                    pool.wait_ge(ve_done, number + 1)
                    pool.tensor_tensor(rstd[:, which], ve[:, which], half[:, :], ALU.pow).then_inc(rstd_done, 1)

                rstd_of(0, 1)
                rstd_of(1, 1)
                with pool.Fori(1, NCH - 1) as n:
                    rstd_of(2 * n, 0)
                    rstd_of(2 * n + 1, 1)
                rstd_of(2 * NCH - 2, 0)
                rstd_of(2 * NCH - 1, 0)

            @block.vector
            def _(dve):
                def statistics(number, which, src):
                    for t in range(TPC):
                        last = dve.bn_stats(stats[:, which, t, :], src[:, t, :])
                    last.then_inc(stats_done, 1)
                    dve.wait_ge(stats_done, number + 1)
                    dve.tensor_copy(seen[:, :], stats[:, which, 0, 0:1])
                    for t in range(TPC):
                        last = dve.bn_aggr(mv[:, which, t, :], stats[:, which, t, :])
                    last.then_inc(mv_done, 1)

                def scale(number, which, dst, src, done):
                    dve.wait_ge(rstd_done, number + 1)
                    for t in range(TPC):
                        last = dve.tensor_scalar(dst[:, t, :], src[:, t, :], mv[:, which, t, 0:1],
                                                 rstd[:, which, t:t + 1], ALU.subtract, ALU.mult)
                    last.then_inc(done, 1)

                def transposed_lo(n, e, k):
                    dve.wait_ge(tr_hi, KT * n + k + 1)
                    dve.tensor_tensor(xT[:, e, 1, k, :], pt[:, :], xT[:, e, 0, k, :].bitcast(F32), ALU.subtract
                                      ).then_inc(tr_lo, 1)

                def post_stats(n, number):
                    dve.wait_ge(y_read, TPC * n + TPC + START)
                    statistics(number, 0, work)

                def post_residual(n, e, number):
                    scale(number, 0, work, work, y_normed)
                    dve.wait_ge(y_normed, n + 1)
                    dve.tensor_tensor(work[:, :, :], work[:, :, :], xin[:, e], ALU.add).then_inc(y_final, 1)

                def chunk(i, e, first, last):
                    n = 2 * i + e
                    number = 2 * n
                    for f in range(NF + 1):
                        F = NF * n + f
                        s = f % 2
                        if f < NF:
                            dve.wait_ge(arg_done, F + 1)
                            dve.tensor_scalar(whole[:, s, :], arg[:, s, :], ROUND, -ROUND, ALU.add, ALU.add
                                              ).then_inc(whole_done, 1)
                            dve.wait_ge(whole_done, F + 1)
                            dve.tensor_tensor(whole[:, s, :], arg[:, s, :], whole[:, s, :], ALU.subtract
                                              ).then_inc(frac_done, 1)
                        if f >= 1:
                            r = (f - 1) % AR
                            dve.wait_ge(act_hi, F)
                            dve.tensor_tensor(act_r[:, r, 1, :], arg[:, 1 - s, :], act_r[:, r, 0, :].bitcast(F32),
                                              ALU.subtract).then_inc(act_lo, 1)
                        if f < NF:
                            dve.wait_ge(sin_done, F + 1)
                            dve.scalar_tensor_tensor(whole[:, s, :], arg[:, s, :], coef[:, f:f + 1], ph[:, f % HB, :],
                                                     ALU.mult, ALU.add).then_inc(q_done, 1)
                        if f == POST_AT[0] and not first:
                            post_stats(n - 1, number)
                        if f == POST_AT[1] and not first:
                            post_residual(n - 1, 1 - e, number)
                        if f == STATS_AT and not last:
                            dve.wait_ge(x_loaded[1 - e], 16 * (i + 1 + e))
                            statistics(number + 1, 1, xin[:, 1 - e])
                        if f == APPLY_AT and not last:
                            if not first:
                                dve.wait_ge(y_stored, 16 * n + START)
                            scale(number + 1, 1, work, xin[:, 1 - e], normed)
                        if f in TR_AT and not last:
                            transposed_lo(n + 1, 1 - e, TR_AT[f])
                    if not last:
                        dve.wait_ge(tr_done, KT * (n + 2))
                    else:
                        dve.wait_ge(y_stored, 16 * n + START)
                    for t in range(TPC):
                        dve.wait_ge(w2_done, TPC * n + t + 1 + START)
                        dve.tensor_tensor(work[:, t, :], py[:, t, :], b2s[:, :], ALU.add).then_inc(y_read, 1)

                for s in (q_done, y_read, act_lo):
                    dve.sem_inc(s, START)
                dve.wait_ge(x_loaded[0], 16)
                statistics(0, 1, xin[:, 0])
                scale(0, 1, work, xin[:, 0], normed)
                for k in range(KT):
                    transposed_lo(0, 0, k)
                chunk(0, 0, True, False)
                chunk(0, 1, False, False)
                with dve.Fori(1, BATCH - 1) as i:
                    for e in range(2):
                        chunk(i, e, False, False)
                for e in range(2):
                    chunk(BATCH - 1, e, False, e == 1)
                post_stats(NCH - 1, 2 * NCH - 1)
                post_residual(NCH - 1, 1, 2 * NCH - 1)

            @block.scalar
            def _(act):
                def transposed_hi(n, e, k):
                    act.wait_ge(tr_done, KT * n + k + 1)
                    act.activation(xT[:, e, 0, k, :], pt[:, :], ACT.Copy).then_inc(tr_hi, 1)

                def chunk(i, e, last):
                    n = 2 * i + e
                    for f in range(NF + 1):
                        F = NF * n + f
                        s = f % 2
                        if f < NF:
                            act.wait_ge(h_done, F + 1)
                            act.wait_ge(act_lo, NF * n + max(f - 1, 0) + START)
                            act.activation(arg[:, s, :], ph[:, f % HB, :], ACT.Identity, bias=turn0[:, f:f + 1],
                                           scale=SLOPE / TWO_PI).then_inc(arg_done, 1)
                        if f >= 1:
                            r = (f - 1) % AR
                            act.wait_ge(q_done, F + START)
                            act.activation(arg[:, 1 - s, :], whole[:, 1 - s, :], ACT.Relu,
                                           bias=vec[:, 0, f - 1:f]).then_inc(relu_done, 1)
                            if f - 1 >= AR:
                                act.wait_ge(w2_used, (NF - 1) * n + f - AR)
                            else:
                                act.wait_ge(w2_done, TPC * n + START)
                            act.wait_ge(relu_done, F)
                            act.activation(act_r[:, r, 0, :], arg[:, 1 - s, :], ACT.Copy).then_inc(act_hi, 1)
                        if f < NF:
                            act.wait_ge(frac_done, F + 1)
                            act.activation(arg[:, s, :], whole[:, s, :], ACT.Sin, scale=TURN).then_inc(sin_done, 1)
                        if f in TR_AT and not last:
                            transposed_hi(n + 1, 1 - e, TR_AT[f])

                for k in range(KT):
                    transposed_hi(0, 0, k)
                with act.Fori(0, BATCH - 1) as i:
                    for e in range(2):
                        chunk(i, e, False)
                for e in range(2):
                    chunk(BATCH - 1, e, e == 1)

            @block.tensor
            def _(pe):
                def transposes(n, e, k, first=False):
                    if not (first and k == 0):
                        pe.wait_ge(tr_lo, KT * n + k)
                    if k == 0:
                        pe.wait_ge(normed, n + 1)
                    for t in range(TPC):
                        last = pe.transpose(pt[:, t * P:(t + 1) * P], work[:, t, k * P:(k + 1) * P], ident[:, :])
                    last.then_inc(tr_done, 1)

                def hidden(n, e, f):
                    pe.wait_ge(q_done, NF * n + (f - HB + 1 if f >= HB else 0) + START)
                    if f == 0:
                        pe.wait_ge(tr_lo, KT * n + KT)
                    terms = [(k, a, b) for k in range(KT) for a, b in PASSES]
                    for j, (k, a, b) in enumerate(terms):
                        last = pe.matmul(ph[:, f % HB, :], w1s[:, a, k, f * P:(f + 1) * P], xT[:, e, b, k, :],
                                         start=(j == 0), stop=(j == len(terms) - 1))
                    last.then_inc(h_done, 1)

                def output(n, f):
                    pe.wait_ge(act_lo, NF * n + f + 1 + START)
                    if f == 0:
                        pe.wait_ge(y_read, TPC * n + START)
                    for t in range(TPC):
                        for j, (a, b) in enumerate(PASSES):
                            last = pe.matmul(py[:, t, :], act_r[:, f % AR, b, t * P:(t + 1) * P], w2s[:, a, f, :],
                                             start=(f == 0 and j == 0), stop=(f == NF - 1 and j == len(PASSES) - 1))
                        if f == NF - 1:
                            last.then_inc(w2_done, 1)
                    if f < NF - 1:
                        last.then_inc(w2_used, 1)

                def chunk(i, e, last):
                    n = 2 * i + e
                    for f in range(NF + 2):
                        if f < NF:
                            hidden(n, e, f)
                        if f in TR_AT and not last:
                            transposes(n + 1, 1 - e, TR_AT[f])
                        if f >= 2:
                            output(n, f - 2)

                pe.sem_inc(w2_done, START)
                for k in range(KT):
                    transposes(0, 0, k, first=True)
                with pe.Fori(0, BATCH - 1) as i:
                    for e in range(2):
                        chunk(i, e, False)
                for e in range(2):
                    chunk(BATCH - 1, e, e == 1)


def layer(nc, x, w_qvk, w_o, w1, b1, phases, w_real, w_imag, w2, b2, out):
    qk_parts = nc.dram_tensor("qk_parts", [BATCH, 2 * GROUPS, 2, P, SEQ], F32, kind="Internal").ap()
    v_rows = nc.dram_tensor("v_rows", [BATCH, SEQ, D], F32, kind="Internal").ap()
    x1 = nc.dram_tensor("x1", [BATCH + 1, SEQ, D], F32, kind="Internal").ap()
    qkv_phase(nc, x, w_qvk, qk_parts, v_rows)
    attention_phase(nc, x, w_o, qk_parts, v_rows, x1)
    ffn_phase(nc, x1, w1, b1, phases, w_real, w_imag, w2, b2, out)


_INS = ["L0_attn_h", "L0_attn_Wqvk", "L0_attn_Wo", "L0_ffn_W1", "L0_ffn_b1", "L0_ffn_quantum_phases",
        "L0_ffn_quantum_weights_real", "L0_ffn_quantum_weights_imag", "L0_ffn_W2", "L0_ffn_b2"]
_OUTS = [((BATCH, SEQ, D), "float32")]


def kernel(**inputs):
    import numpy as _np
    import concourse.bacc as _bacc
    from concourse import mybir as _mybir
    from concourse.bass_utils import run_bass_kernel_spmd as _run

    nc = _bacc.Bacc("TRN2", target_bir_lowering=False, num_devices=1)
    arrays, args = {}, []
    for name in _INS:
        a = _np.ascontiguousarray(inputs[name])
        arrays[f"in_{name}_dram"] = a
        args.append(nc.dram_tensor(f"in_{name}_dram", a.shape, _mybir.dt.from_np(a.dtype), kind="ExternalInput").ap())
    for i, (shape, dtype) in enumerate(_OUTS):
        dt = _mybir.dt.from_np(_np.dtype(dtype))
        args.append(nc.dram_tensor(f"out_{i}_dram", shape, dt, kind="ExternalOutput").ap())
    layer(nc, *args)
    r = _run(nc, [arrays], core_ids=[0])
    got = tuple(r.results[0][f"out_{i}_dram"] for i in range(len(_OUTS)))
    return got[0]
```

```python
import math
from contextlib import ExitStack

import concourse.bass as bass
from concourse import mybir

F32 = mybir.dt.float32
F32R = mybir.dt.float32r
BF16 = mybir.dt.bfloat16
F16 = mybir.dt.float16
ALU = mybir.AluOpType
ACT = mybir.ActivationFunctionType
AX_X = mybir.AxisListType.X

P = 128
BATCH, SEQ, D = 8, 1024, 512
HEADS, HD = 16, 32
FF = 2048
CH = 512
TPC = CH // P
KT = D // P
CPB = SEQ // CH
NCH = BATCH * CPB
HPG = P // HD
GROUPS = HEADS // HPG
EPS = 1e-5
VP = 3
VF = HD + 1
VH = VP * VF
VROW = HEADS * VH
START = 1
MASKED = -1e30
PASSES = ((0, 0), (0, 1), (1, 0))


def split_weights(block, loads, raw, sem_loaded, sem_hi, sem_lo, after_loads=None, before_loads=None,
                  last_scalar=None, first_vector=None):
    R = len(raw)

    @block.sync
    def _(sp):
        if before_loads:
            before_loads(sp)
        for n, (src, _at) in enumerate(loads):
            if n >= R:
                sp.wait_ge(sem_lo, n - R + 1)
            sp.dma_start(raw[n % R], src).then_inc(sem_loaded[n % R], 16)
        if after_loads:
            after_loads(sp)

    @block.scalar
    def _(act):
        for n, (_src, at) in enumerate(loads):
            act.wait_ge(sem_loaded[n % R], 16 * (n // R + 1))
            act.activation(at(0), raw[n % R], ACT.Copy).then_inc(sem_hi, 1)
        if last_scalar:
            last_scalar(act)

    @block.vector
    def _(dve):
        if first_vector:
            first_vector(dve)
        for n, (_src, at) in enumerate(loads):
            dve.wait_ge(sem_hi, n + 1)
            dve.tensor_tensor(at(1), raw[n % R], at(0).bitcast(F32), ALU.subtract).then_inc(sem_lo, 1)


def identity_matrix(pool, tile, sem):
    pool.memset(tile, 0.0).then_inc(sem, 1)
    pool.wait_ge(sem, 1)
    pool.affine_select(out=tile, in_=tile, compare_op=ALU.not_equal, fill=1.0, base=0,
                       pattern=[[-1, P]], channel_multiplier=1).then_inc(sem, 1)


def qkv_phase(nc, x, w_qvk, qk_parts, v_parts):
    MM = 12
    QK = 8
    BANKS = 6
    STAGE = 4
    SCHED = [("mm", m) for m in range(6)] + [("tr", 0), ("mm", 6), ("tr", 1), ("mm", 7), ("tr", 2), ("mm", 8),
                                             ("tr", 3), ("mm", 9), ("mm", 10), ("mm", 11)]
    ctx = ExitStack()
    with ctx:
        def sb(name, shape, dt=F32):
            return ctx.enter_context(nc.sbuf_tensor(name, shape, dt))

        def sem(name):
            return ctx.enter_context(nc.semaphore("q_" + name))

        w = sb("q_w", [P, 2, KT, 3 * D], F32R)
        raw = sb("q_raw", [P, KT, 3 * D])
        xin = sb("q_x", [P, 2, TPC, D])
        xT = sb("q_xT", [P, 2, 2, KT, CH], F32R)
        stats = sb("q_stats", [P, 2, TPC, 6])
        seen = sb("q_seen", [P, 1])
        mv = sb("q_mv", [P, 2, TPC, 2])
        ve = sb("q_ve", [P, 2, TPC])
        rstd = sb("q_rstd", [P, 2, TPC])
        half = sb("q_half", [P, TPC])
        eps = sb("q_eps", [P, TPC])
        ident = sb("q_ident", [P, P])
        stage = sb("q_stage", [P, STAGE, 2, CH], F32R)
        vstage = sb("q_vstage", [P, TPC, HEADS, VP, VF], BF16)
        vrest = sb("q_vrest", [P, 2, HEADS, HD])
        zeros = sb("q_zeros", [P, HEADS, HD])
        pt = ctx.enter_context(nc.psum_tensor("q_pt", [P, 2, CH], F32))
        pm = ctx.enter_context(nc.psum_tensor("q_pm", [P, BANKS, CH], F32))

        w_loaded = [sem(f"w_loaded{n}") for n in range(KT)]
        w_hi, w_lo = sem("w_hi"), sem("w_lo")
        ident_set, half_set = sem("ident_set"), sem("half_set")
        x_loaded = [sem(f"x_loaded{e}") for e in range(2)]
        stats_done, mv_done, normed = sem("stats_done"), sem("mv_done"), sem("normed")
        ve_done, rstd_done = sem("ve_done"), sem("rstd_done")
        tr_done, tr_hi, tr_lo = sem("tr_done"), sem("tr_hi"), sem("tr_lo")
        mm_done, qk_hi, qk_lo = sem("mm_done"), sem("qk_hi"), sem("qk_lo")
        v_first, v_rest, v_second, v_out = sem("v_first"), sem("v_rest"), sem("v_second"), sem("v_out")
        stored = [sem(f"stored{n}") for n in range(STAGE)]
        v_stored = sem("v_stored")
        x_v = x.rearrange("b (c t p) d -> (b c) p t d", p=P, t=TPC)

        with nc.Block() as wblock:
            def first_chunks(sp):
                for e in range(2):
                    sp.dma_start(xin[:, e], x_v[e]).then_inc(x_loaded[e], 16)

            split_weights(wblock, [(w_qvk[k * P:(k + 1) * P, :], (lambda part, k=k: w[:, part, k, :]))
                                   for k in range(KT)], [raw[:, k] for k in range(KT)], w_loaded, w_hi, w_lo,
                          first_chunks)

            @wblock.gpsimd
            def _(pool):
                identity_matrix(pool, ident[:, :], ident_set)
                pool.memset(half[:, :], -0.5).then_inc(half_set, 1)
                pool.memset(eps[:, :], EPS).then_inc(half_set, 1)
                pool.memset(zeros[:, :, :], 0.0).then_inc(half_set, 1)
                pool.memset(vstage[:, :, :, 0, HD:VF], 1.0).then_inc(half_set, 1)
                pool.memset(vstage[:, :, :, 1:VP, HD:VF], 0.0).then_inc(half_set, 1)

        with nc.Block() as block:
            @block.sync
            def _(sp):
                def load(n, e):
                    sp.dma_start(xin[:, e], x_v[n]).then_inc(x_loaded[e], 16)

                def store(i, e):
                    n = 2 * i + e
                    for m in range(QK):
                        sp.wait_ge(qk_lo, QK * n + m + 1 + QK)
                        sp.dma_start(qk_parts[i, m].rearrange("l p t -> p l t")[:, :, e * CH:(e + 1) * CH],
                                     stage[:, m % STAGE].bitcast(F32)).then_inc(stored[m % STAGE], 16)
                    sp.wait_ge(v_out, TPC * n + TPC + TPC)
                    sp.dma_start(v_parts[i].rearrange("(c t p) f -> c p t f", p=P, t=TPC)[e],
                                 vstage[:, :, :, :, :].rearrange("p t h a f -> p t (h a f)")).then_inc(v_stored, 16)

                for s in (*stored, v_stored):
                    sp.sem_inc(s, START)
                with sp.Fori(0, BATCH - 1) as i:
                    for e in range(2):
                        sp.wait_ge(tr_done, KT * (2 * i + e) + KT)
                        load(2 * i + e + 2, e)
                        store(i, e)
                for e in range(2):
                    store(BATCH - 1, e)
                for s in stored:
                    sp.wait_ge(s, 16 * (QK // STAGE) * NCH + START)
                sp.wait_ge(v_stored, 16 * NCH + START)

            @block.gpsimd
            def _(pool):
                def rstd_of(n, e):
                    pool.wait_ge(mv_done, n + 1)
                    pool.tensor_tensor(ve[:, e], mv[:, e, :, 1], eps[:, :], ALU.add).then_inc(ve_done, 1)
                    pool.wait_ge(ve_done, n + 1)
                    pool.tensor_tensor(rstd[:, e], ve[:, e], half[:, :], ALU.pow).then_inc(rstd_done, 1)

                def v_low_parts(n):
                    for t in range(TPC):
                        m = TPC * n + t
                        pool.wait_ge(v_rest, m + 1 + TPC)
                        pool.tensor_tensor(vstage[:, t, :, 1, 0:HD], vrest[:, t % 2], zeros[:, :, :], ALU.add
                                           ).then_inc(v_second, 1)
                        pool.wait_ge(v_second, m + 1)
                        pool.tensor_tensor(vstage[:, t, :, 2, 0:HD], vrest[:, t % 2], vstage[:, t, :, 1, 0:HD],
                                           ALU.subtract).then_inc(v_out, 1)

                rstd_of(0, 0)
                with pool.Fori(0, BATCH - 1) as i:
                    for e in range(2):
                        rstd_of(2 * i + e + 1, 1 - e)
                        v_low_parts(2 * i + e)
                rstd_of(NCH - 1, 1)
                for n in (NCH - 2, NCH - 1):
                    v_low_parts(n)

            @block.vector
            def _(dve):
                dve.sem_inc(qk_lo, QK)
                dve.sem_inc(v_rest, TPC)

                def ln_stats(n, e, turn):
                    dve.wait_ge(x_loaded[e], 16 * turn)
                    for t in range(TPC):
                        last = dve.bn_stats(stats[:, e, t, :], xin[:, e, t, :])
                    last.then_inc(stats_done, 1)
                    dve.wait_ge(stats_done, n + 1)
                    dve.tensor_copy(seen[:, 0:1], stats[:, e, 0, 0:1])
                    for t in range(TPC):
                        last = dve.bn_aggr(mv[:, e, t, :], stats[:, e, t, :])
                    last.then_inc(mv_done, 1)

                def ln_apply(n, e):
                    dve.wait_ge(rstd_done, n + 1)
                    for t in range(TPC):
                        last = dve.tensor_scalar(xin[:, e, t, :], xin[:, e, t, :], mv[:, e, t, 0:1],
                                                 rstd[:, e, t:t + 1], ALU.subtract, ALU.mult)
                    last.then_inc(normed, 1)

                def transposed_lo(n, e, k):
                    dve.wait_ge(tr_hi, KT * n + k + 1)
                    dve.tensor_tensor(xT[:, e, 1, k, :], pt[:, k % 2, :], xT[:, e, 0, k, :].bitcast(F32),
                                      ALU.subtract).then_inc(tr_lo, 1)

                def chunk(i, e, last):
                    n = 2 * i + e
                    if not last:
                        ln_stats(n + 1, 1 - e, i + 1 + e)
                    for kind, m in SCHED:
                        if kind == "tr":
                            if not last:
                                transposed_lo(n + 1, 1 - e, m)
                        elif m < QK:
                            dve.wait_ge(qk_hi, QK * n + m + 1)
                            dve.tensor_tensor(stage[:, m % STAGE, 1], pm[:, m % BANKS, :],
                                              stage[:, m % STAGE, 0].bitcast(F32), ALU.subtract).then_inc(qk_lo, 1)
                        else:
                            t = m - QK
                            dve.wait_ge(v_first, TPC * n + t + 1)
                            dve.wait_ge(v_out, TPC * n + t - 1 + TPC)
                            dve.tensor_tensor(vrest[:, t % 2], pm[:, m % BANKS, :].rearrange("p (h f) -> p h f", f=HD),
                                              vstage[:, t, :, 0, 0:HD], ALU.subtract).then_inc(v_rest, 1)
                        if kind == "mm" and m == 2 and not last:
                            ln_apply(n + 1, 1 - e)

                ln_stats(0, 0, 1)
                ln_apply(0, 0)
                for k in range(KT):
                    transposed_lo(0, 0, k)
                with dve.Fori(0, BATCH - 1) as i:
                    for e in range(2):
                        chunk(i, e, False)
                for e in range(2):
                    chunk(BATCH - 1, e, e == 1)

            @block.scalar
            def _(act):
                act.sem_inc(v_out, TPC)

                def transposed_hi(n, e, k):
                    act.wait_ge(tr_done, KT * n + k + 1)
                    act.activation(xT[:, e, 0, k, :], pt[:, k % 2, :], ACT.Copy).then_inc(tr_hi, 1)

                def chunk(i, e, last):
                    n = 2 * i + e
                    for kind, m in SCHED:
                        if kind == "tr":
                            if not last:
                                transposed_hi(n + 1, 1 - e, m)
                            continue
                        act.wait_ge(mm_done, MM * n + m + 1)
                        if m < QK:
                            act.wait_ge(stored[m % STAGE], 16 * (2 * n + m // STAGE) + START)
                            act.activation(stage[:, m % STAGE, 0], pm[:, m % BANKS, :], ACT.Copy).then_inc(qk_hi, 1)
                        else:
                            if m == QK:
                                act.wait_ge(v_stored, 16 * n + START)
                            act.activation(vstage[:, m - QK, :, 0, 0:HD],
                                           pm[:, m % BANKS, :].rearrange("p (h f) -> p h f", f=HD), ACT.Copy
                                           ).then_inc(v_first, 1)

                for k in range(KT):
                    transposed_hi(0, 0, k)
                with act.Fori(0, BATCH - 1) as i:
                    for e in range(2):
                        chunk(i, e, False)
                for e in range(2):
                    chunk(BATCH - 1, e, e == 1)

            @block.tensor
            def _(pe):
                def transposes(n, e, k, first=False):
                    if not (first and k < 2):
                        pe.wait_ge(tr_lo, KT * n + k - 1)
                    if k == 0:
                        pe.wait_ge(normed, n + 1)
                    for t in range(TPC):
                        last = pe.transpose(pt[:, k % 2, t * P:(t + 1) * P], xin[:, e, t, k * P:(k + 1) * P], ident[:, :])
                    last.then_inc(tr_done, 1)

                def output(n, e, m):
                    before = m - BANKS
                    if 0 <= before:
                        pe.wait_ge(qk_lo, QK * n + before + 1 + QK)
                    elif before + MM < QK:
                        pe.wait_ge(qk_lo, QK * n + before + MM + 1)
                    else:
                        pe.wait_ge(v_rest, TPC * n + before + MM - QK + 1)
                    if m == 0:
                        pe.wait_ge(tr_lo, KT * n + KT)
                    terms = [(k, a, b) for k in range(KT) for a, b in PASSES]
                    for j, (k, a, b) in enumerate(terms):
                        if m < QK:
                            col = m * P if m < GROUPS else 2 * D + (m - GROUPS) * P
                            lhs, rhs = w[:, a, k, col:col + P], xT[:, e, b, k, :]
                        else:
                            lhs, rhs = xT[:, e, b, k, (m - QK) * P:(m - QK + 1) * P], w[:, a, k, D:2 * D]
                        last = pe.matmul(pm[:, m % BANKS, :], lhs, rhs, start=(j == 0), stop=(j == len(terms) - 1))
                    last.then_inc(mm_done, 1)

                def chunk(i, e, last):
                    n = 2 * i + e
                    for kind, m in SCHED:
                        if kind == "mm":
                            output(n, e, m)
                        elif not last:
                            transposes(n + 1, 1 - e, m)

                for k in range(KT):
                    transposes(0, 0, k, first=True)
                with pe.Fori(0, BATCH - 1) as i:
                    for e in range(2):
                        chunk(i, e, False)
                for e in range(2):
                    chunk(BATCH - 1, e, e == 1)


QT = SEQ // P
QC = 256
TQ = QC // P
NC = SEQ // QC
STEPS = [(c, j) for c in range(NC) for j in range(TQ * (c + 1))]
NS = len(STEPS)
LAST_OF_C = [max(k for k, (c, _j) in enumerate(STEPS) if c == cc) for cc in range(NC)]
UNITS = GROUPS


def score_pieces():
    out = []
    for i in range(QT):
        for half in range(i // TPC + 1):
            n = min((i + 1) * P - half * CH, CH)
            per = CH // n
            out += [(i, half, list(range(h, h + per)), n) for h in range(0, HPG, per)]
    return out


LAG = 6
TURN_AT = [k + LAG + 2 for k in LAST_OF_C]
PIECES = score_pieces()
PIECES_AT = dict(enumerate((3, 3, 3, 2, 2, 2, 1, 2, 2, 3, 2, 2, 2, 2, 2, 3, 2)))
MAX_AT = 17
V_FREE_AT = LAG + 1
Q_FREE_AT = LAST_OF_C[CH // QC - 1] + 1
K_FREE_AT = max(k for k, (_c, j) in enumerate(STEPS) if j < TPC) + 1
WO_AT = list(range(10, 10 + 4 * QT, 2))
WO_AT_LAST = [10, 11, 12, 13, 14, 15, 16, 17, 19, 20, 21, 22, 28, 29, 30, 31]
DH = D // 2
WO_SMALL, WO_NORM, WO_ADD, WO_STORE = 1, 2, 3, 4
TAIL = WO_AT_LAST[-1] + WO_STORE + 1 - NS
assert sum(PIECES_AT.values()) == len(PIECES)
FIRST_OF_SECOND = next(m for m, (i, _half, _heads, _n) in enumerate(PIECES) if i >= TPC)


class Stage:

    def __init__(self, before, this, after):
        self.before, self.this, self.after = before, this, after
        self.wo_at = (WO_AT if after else WO_AT_LAST, WO_AT if this else WO_AT_LAST)
        self.slots = [(u, k) for u in range(UNITS if this else 1) for k in range(NS if this else TAIL)]
        self.work = self.shared_work()

    def earlier(self, u, k, lag):
        s = u * NS + k - lag
        if s < 0:
            return (s // NS, s % NS) if self.before else None
        return (s // NS, s % NS) if self.this else None

    def tiles(self, u, k, lag):
        return [(b, m // 2) for b, m in self.halves(u, k, lag) if m % 2]

    def halves(self, u, k, lag):
        s = u * NS + k - lag
        for m, (this, before) in enumerate(zip(*self.wo_at)):
            if s == this + (UNITS - 1) * NS and self.this:
                yield 0, m
            if s == before - NS and self.before:
                yield -1, m

    def shared_work(self):
        out = []
        for u, k in self.slots:
            if self.this and (u < UNITS - 1 or self.after):
                n = sum(PIECES_AT.get(kk, 0) for kk in range(k))
                out += [(u, k, "piece", u + 1, m) for m in range(n, n + PIECES_AT.get(k, 0))]
                if k == MAX_AT:
                    out.append((u, k, "max", u + 1, 0))
            for c, at in enumerate(TURN_AT):
                e = self.earlier(u, k, at)
                if e and e[1] == 0:
                    out.append((u, k, "turn", e[0], c))
            out += [(u, k, "wo", b, m) for b, m in self.halves(u, k, 0)]
        return out

    def at(self, u, k):
        return [(n, what, unit, m) for n, (uu, kk, what, unit, m) in enumerate(self.work) if (uu, kk) == (u, k)]


FIRST, MIDDLE, LAST, DRAIN = Stage(False, True, True), Stage(True, True, True), Stage(True, True, False), \
    Stage(True, False, False)
AHEAD = [("piece", m) for m in range(len(PIECES))] + [("max", 0)]


def work_before(i, stage):
    if stage is FIRST:
        return len(AHEAD)
    n = len(AHEAD) + len(FIRST.work) - len(MIDDLE.work)
    if stage is DRAIN:
        n += len(LAST.work) - len(MIDDLE.work)
    return n + len(MIDDLE.work) * i


assert len(MIDDLE.work) % 2 == 0


def wait(engine, sem, count):
    if not (isinstance(count, int) and count <= 0):
        engine.wait_ge(sem, count)


def attention_phase(nc, x, w_o, qk_parts, v_parts, x1):
    SCALE = 1.0 / math.sqrt(D)
    KQ = 3 * HD
    KM = KQ + 2
    PR, HR, YR = 5, 10, 4
    LIFT = 8 * math.log(2)

    ctx = ExitStack()
    with ctx:
        def sb(name, shape, dt=F32):
            return ctx.enter_context(nc.sbuf_tensor("a_" + name, shape, dt))

        def ps(name, shape):
            return ctx.enter_context(nc.psum_tensor("a_" + name, shape, F32))

        def sem(name):
            return ctx.enter_context(nc.semaphore("a_" + name))

        wo = sb("wo", [P, 2, KT, D], F32R)
        qp = [sb(f"qp{b}", [KM, HPG, SEQ], F32R) for b in range(2)]
        kp = [sb(f"kp{b}", [KM, HPG, SEQ], F32R) for b in range(2)]
        vt = sb("vt", [P, 2, QT, HPG * VH], BF16)
        prob = sb("prob", [P, PR, HPG, QC])
        prob_hi = sb("prob_hi", [P, HR, HPG, QC], F16)
        prob_lo = sb("prob_lo", [P, HR, HPG, QC], F16)
        lift = sb("lift", [P, 1])
        ident = sb("ident", [P, P])
        identb, mask_q, mask_k = (sb(n, [P, P], BF16) for n in ("identb", "mask_q", "mask_k"))
        mx = sb("mx", [P, HPG, QT])
        mx2 = sb("mx2", [P, HPG, QT - TPC])
        nm = sb("nm", [HPG * QT, 2, P], F32R)
        osum = sb("osum", [P, TQ, HPG, VF])
        rden = sb("rden", [P, TQ, HPG])
        o = sb("o", [P, 2, TQ, P])
        oT = sb("oT", [P, 2, GROUPS, SEQ], F32R)
        stats = sb("stats", [P, YR, 2, 6])
        seen = sb("seen", [P, 1])
        mv = sb("mv", [P, YR, 2])
        small = sb("small", [P, YR, 4])
        half = sb("half", [P, 1])
        eps = sb("eps", [P, 1])
        minus = sb("minus", [P, 1])
        y = sb("y", [P, YR, D])
        xr = sb("xr", [P, 2, D])
        pw = ps("pw", [P, 2, CH])
        pst = ps("pst", [P, 2, HPG, QC])
        acc = ps("acc", [P, TQ, CH])

        w_loaded = [sem(f"w_loaded{n}") for n in range(KT)]
        w_hi, w_lo = sem("w_hi"), sem("w_lo")
        const = sem("const")
        qk_loaded = [[sem(f"qk_loaded{b}{c}") for c in range(CPB)] for b in range(2)]
        v_loaded = [sem(f"v_loaded{b}") for b in range(2)]
        work_done, released = sem("work_done"), sem("released")
        max_ready, nm_hi, nm_stored = sem("max_ready"), sem("nm_hi"), sem("nm_stored")
        st_done, exp_done, hi_done = sem("st_done"), sem("exp_done"), sem("hi_done")
        lo_done, pv_done = sem("lo_done"), sem("pv_done")
        acc_read, rden_done, o_done, oT_hi = sem("acc_read"), sem("rden_done"), sem("o_done"), sem("oT_hi")
        stats_done, mv_done, small_done = sem("stats_done"), sem("mv_done"), sem("small_done")
        xr_loaded = [sem(f"xr_loaded{b}") for b in range(2)]
        y_norm, y_done = sem("y_norm"), sem("y_done")
        y_stored = [sem(f"y_stored{b}") for b in range(YR)]

        x_v = x.rearrange("b (t p) d -> b t p d", p=P)

        def load_qk(sp, i, u, c, q):
            i, g, b = i + u // UNITS, u % UNITS, u % 2
            m = g if q else GROUPS + g
            for term, part in enumerate((0, 1, 0) if q else (0, 0, 1)):
                sp.dma_start((qp if q else kp)[b][term * HD:(term + 1) * HD, :, c * CH:(c + 1) * CH].bitcast(F32),
                             qk_parts[i, m, part].rearrange("(h r) t -> r h t", r=HD)[:, :, c * CH:(c + 1) * CH]
                             ).then_inc(qk_loaded[b][c], 16)

        def load_v(sp, i, u):
            i, g, b = i + u // UNITS, u % UNITS, u % 2
            sp.dma_start(vt[:, b], v_parts[i].rearrange("(j p) f -> p j f", p=P)
                         [:, :, g * HPG * VH:(g + 1) * HPG * VH]).then_inc(v_loaded[b], 16)

        def load_x(sp, i, t):
            sp.dma_start(xr[:, t % 2, :], x_v[i, t]).then_inc(xr_loaded[t % 2], 16)

        with nc.Block() as wblock:
            def first_units(sp):
                for u in range(2):
                    for c in range(CPB):
                        load_qk(sp, 0, u, c, True)
                        load_qk(sp, 0, u, c, False)
                    load_v(sp, 0, u)
                load_x(sp, 0, 0)
                load_x(sp, 0, 1)

            split_weights(wblock, [(w_o[k * P:(k + 1) * P, :], (lambda part, k=k: wo[:, part, k, :]))
                                   for k in range(KT)],
                          [prob[:, k, :, :].rearrange("p h q -> p (h q)")[:, 0:D] for k in range(KT)],
                          w_loaded, w_hi, w_lo, first_units)

            @wblock.gpsimd
            def _(pool):
                identity_matrix(pool, ident[:, :], const)
                pool.memset(identb[:, :], 0.0).then_inc(const, 1)
                pool.memset(mask_q[:, :], 0.0).then_inc(const, 1)
                pool.memset(mask_k[:, :], 0.0).then_inc(const, 1)
                pool.wait_ge(const, 5)
                pool.affine_select(out=identb[:, :], in_=identb[:, :], compare_op=ALU.not_equal, fill=1.0, base=0,
                                   pattern=[[-1, P]], channel_multiplier=1)
                pool.affine_select(out=mask_q[:, :], in_=mask_q[:, :], compare_op=ALU.is_ge, fill=MASKED, base=0,
                                   pattern=[[-1, P]], channel_multiplier=1)
                pool.affine_select(out=mask_k[:, :], in_=mask_k[:, :], compare_op=ALU.is_ge, fill=MASKED, base=0,
                                   pattern=[[1, P]], channel_multiplier=-1)
                pool.memset(half[:, :], -0.5)
                pool.memset(eps[:, :], EPS)
                pool.memset(minus[:, :], -1.0)
                pool.memset(lift[:, :], LIFT).then_inc(const, 1)
                for b in range(2):
                    pool.wait_ge(const, 6 + b)
                    pool.memset(kp[b][KQ:KM, :, :].bitcast(F32), 1.0).then_inc(const, 1)

        with nc.Block() as block:
            def first_query(k):
                c, j = STEPS[k]
                return P * max(0, j - TQ * c)

            def run_all(engine, run):
                run(0, FIRST)
                with engine.Fori(1, BATCH - 1) as i:
                    run(i, MIDDLE)
                run(BATCH - 1, LAST)
                run(BATCH, DRAIN)

            @block.sync
            def _(sp):
                x1_v = x1.rearrange("b (t p) d -> b t p d", p=P)

                def store_max(b):
                    for part in range(2):
                        sp.dma_start(qp[b][KQ + part:KQ + part + 1, :, :].bitcast(F32), nm[:, part, :].bitcast(F32)
                                     ).then_inc(nm_stored, 16)

                def run(i, stage):
                    for u, k in stage.slots:
                        v = UNITS * i + u
                        if k == 0 and stage.this and (u < UNITS - 1 or stage.after) and not (stage is FIRST and u == 0):
                            sp.wait_ge(st_done, NS * v)
                            load_qk(sp, i, u + 1, 1, True)
                            load_qk(sp, i, u + 1, 1, False)
                        if k == V_FREE_AT and stage.this and (u < UNITS - 1 or stage.after) and \
                                not (stage is FIRST and u == 0):
                            sp.wait_ge(pv_done, NS * v)
                            load_v(sp, i, u + 1)
                        if k == Q_FREE_AT and stage.this and (u < UNITS - 2 or stage.after):
                            sp.wait_ge(st_done, NS * v + Q_FREE_AT)
                            load_qk(sp, i, u + 2, 0, True)
                        if k == K_FREE_AT and stage.this and (u < UNITS - 2 or stage.after):
                            sp.wait_ge(st_done, NS * v + K_FREE_AT)
                            load_qk(sp, i, u + 2, 0, False)
                        for b, t in stage.tiles(u, k, WO_STORE):
                            sp.wait_ge(y_done, QT * (i + b) + t + 1)
                            sp.dma_start(x1_v[i + b + 2, t], y[:, t % YR, :]).then_inc(y_stored[t % YR], 16)
                            if t + 2 < QT:
                                load_x(sp, i + b, t + 2)
                            elif stage is not DRAIN:
                                load_x(sp, i + b + 1, t + 2 - QT)
                        if k == MAX_AT:
                            for at, what, unit, _m in stage.at(u, k):
                                if what == "max":
                                    sp.wait_ge(released, work_before(i, stage) + at + 1)
                                    store_max(unit % 2)

                sp.wait_ge(released, len(AHEAD))
                store_max(0)
                run_all(sp, run)
                for s in y_stored:
                    sp.wait_ge(s, 16 * BATCH * QT // YR)

            @block.tensor
            def _(pe):
                def piece(b, bank, m):
                    i, half_, heads, n = PIECES[m]
                    diagonal = half_ == i // TPC
                    for s, h in enumerate(heads):
                        last = pe.matmul(pw[:, bank, s * n:(s + 1) * n], qp[b][0:KQ, h, i * P:(i + 1) * P],
                                         kp[b][0:KQ, h, half_ * CH:half_ * CH + n], start=True, stop=not diagonal)
                        if diagonal:
                            last = pe.matmul(pw[:, bank, (s + 1) * n - P:(s + 1) * n], identb[:, :], mask_q[:, :],
                                             start=False, stop=True)
                    return last

                def shared(i, at, before, what, unit, m, stage):
                    bank = ((before if isinstance(before, int) else work_before(0, stage)) + at) % 2
                    wait(pe, released, before + at - 1)
                    if what == "piece":
                        b = unit % 2
                        if m in (0, FIRST_OF_SECOND):
                            pe.wait_ge(qk_loaded[b][int(m > 0)], 96 * (2 * i + unit // 2 + 1))
                        last = piece(b, bank, m)
                    elif what == "max":
                        pe.wait_ge(max_ready, UNITS * i + unit + 1)
                        last = pe.transpose(pw[0:HPG * QT, bank, 0:P], mx[:, :, :].rearrange("p h i -> p (h i)"),
                                            ident[:, :])
                    elif what == "turn":
                        pe.wait_ge(o_done, NC * (UNITS * i + unit) + m + 1)
                        for t in range(TQ):
                            last = pe.transpose(pw[:, bank, t * P:(t + 1) * P], o[:, m % 2, t, :], ident[:, :])
                    else:
                        if m % (2 * TQ) == 0:
                            turn = next((n for n, it in enumerate(stage.work)
                                         if it[2:] == ("turn", UNITS * unit + UNITS - 1, m // (2 * TQ))), 0)
                            pe.wait_ge(released, before + turn + 1)
                        terms = [(g, a, w) for g in range(GROUPS) for w, a in PASSES]
                        for j, (g, a, w) in enumerate(terms):
                            last = pe.matmul(pw[:, bank, 0:DH], oT[:, a, g, m // 2 * P:(m // 2 + 1) * P],
                                             wo[:, w, g, m % 2 * DH:(m % 2 + 1) * DH],
                                             start=(j == 0), stop=(j == len(terms) - 1))
                    last.then_inc(work_done, 1)

                def scores(i, u, k, heads):
                    c, j = STEPS[k]
                    b, slot, v = u % 2, k % 2, UNITS * i + u
                    if heads[0] == 0:
                        if k == 0:
                            pe.wait_ge(nm_stored, 32 * v + 32)
                        wait(pe, exp_done, NS * v + k - 1)
                    for h in heads:
                        diagonal = j >= TQ * c
                        last = pe.matmul(pst[:, slot, h, :], kp[b][:, h, j * P:(j + 1) * P],
                                         qp[b][:, h, c * QC:(c + 1) * QC], start=True, stop=not diagonal)
                        if diagonal:
                            off = first_query(k)
                            last = pe.matmul(pst[:, slot, h, off:off + P], identb[:, :], mask_k[:, :],
                                             start=False, stop=True)
                    if heads[-1] == HPG - 1:
                        last.then_inc(st_done, 1)

                def weigh(i, u, k, t):
                    c, j = STEPS[k]
                    b, v = u % 2, UNITS * i + u
                    first = first_query(k) // P
                    if t < first:
                        return
                    if t == first:
                        pe.wait_ge(lo_done, NS * v + k + 1)
                        if k == 0:
                            pe.wait_ge(v_loaded[b], 16 * (2 * i + u // 2 + 1))
                    if j == 0:
                        wait(pe, acc_read, TQ * (NC * v + c - 1) + t + 1)
                    for h in range(HPG):
                        for part, skip in ((prob_hi, 0), (prob_lo, VF)):
                            last = pe.matmul(acc[:, t, h * VH + skip:(h + 1) * VH],
                                             part[:, k % HR, h, t * P:(t + 1) * P],
                                             vt[:, b, j, h * VH:(h + 1) * VH - skip],
                                             start=(j == 0 and h == 0 and not skip),
                                             stop=(j == TQ * c + t and h == HPG - 1 and skip > 0))
                    if t == TQ - 1:
                        last.then_inc(pv_done, 1)

                PARTS = 2 + TQ

                def run(i, stage):
                    before = work_before(i, stage)
                    for u, k in stage.slots:
                        e = stage.earlier(u, k, LAG)
                        items = stage.at(u, k)
                        for part in range(PARTS):
                            if part < 2 and stage.this:
                                scores(i, u, k, range(part * HPG // 2, (part + 1) * HPG // 2))
                            if part >= 2 and e:
                                weigh(i, *e, part - 2)
                            for at, what, unit, m in (items[part:part + 1] if part < PARTS - 1 else items[part:]):
                                shared(i, at, before, what, unit, m, stage)

                for at, (what, m) in enumerate(AHEAD):
                    shared(0, at, 0, what, 0, m, None)
                run_all(pe, run)

            @block.scalar
            def _(act):
                def exponentials(i, u, k):
                    v, off = UNITS * i + u, first_query(k)
                    wait(act, lo_done, NS * v + k - PR + 1)
                    act.wait_ge(st_done, NS * v + k + 1)
                    act.activation(prob[:, k % PR, :, off:QC], pst[:, k % 2, :, off:QC], ACT.Exp, scale=SCALE,
                                   bias=lift[:, :]).then_inc(exp_done, 1)

                def high(i, u, k):
                    v, off = UNITS * i + u, first_query(k)
                    act.wait_ge(exp_done, NS * v + k + 1)
                    wait(act, pv_done, NS * v + k - HR + 1)
                    act.activation(prob_hi[:, k % HR, :, off:QC], prob[:, k % PR, :, off:QC], ACT.Copy
                                   ).then_inc(hi_done, 1)

                def wo_norm(i, t):
                    act.wait_ge(small_done, 4 * (QT * i + t) + 4)
                    act.activation(y[:, t % YR, :], y[:, t % YR, :], ACT.Identity, bias=small[:, t % YR, 3:4],
                                   scale=small[:, t % YR, 1:2]).then_inc(y_norm, 1)

                def run(i, stage):
                    for u, k in stage.slots:
                        if stage.this:
                            exponentials(i, u, k)
                        e = stage.earlier(u, k, 1)
                        if e:
                            high(i, *e)
                        for b, t in stage.tiles(u, k, WO_NORM):
                            wo_norm(i + b, t)

                run_all(act, run)

            @block.vector
            def _(dve):
                def maxima(i, at, before, what, unit, m, bank):
                    dve.wait_ge(work_done, before + at + 1)
                    if what == "piece":
                        qt, half_, heads, n = PIECES[m]
                        out = mx2[:, heads[0]:heads[-1] + 1, qt - TPC] if half_ else mx[:, heads[0]:heads[-1] + 1, qt]
                        src = pw[:, bank, 0:n * len(heads)].rearrange("p (h n) -> p h n", n=n)
                        dve.tensor_reduce(out, src, AX_X, ALU.max).then_inc(released, 1)
                        if m == len(PIECES) - 1:
                            dve.wait_ge(released, before + at + 1)
                            dve.tensor_tensor(mx[:, :, TPC:QT], mx[:, :, TPC:QT], mx2[:, :, :], ALU.max
                                              ).then_inc(max_ready, 1)
                    else:
                        v = UNITS * i + unit
                        wait(dve, nm_stored, 32 * v)
                        src = pw[0:HPG * QT, bank, 0:P]
                        dve.tensor_scalar(nm[:, 0, :], src, -1.0, None, ALU.mult).then_inc(nm_hi, 1)
                        dve.wait_ge(nm_hi, v + 1)
                        dve.scalar_tensor_tensor(nm[:, 1, :], src, -1.0, nm[:, 0, :].bitcast(F32), ALU.mult,
                                                 ALU.subtract).then_inc(released, 1)

                def sums(i, u, c, t):
                    dve.wait_ge(pv_done, NS * (UNITS * i + u) + STEPS.index((c, TQ * c + t)) + 1)
                    if t == 0:
                        wait(dve, o_done, NC * (UNITS * i + u) + c)
                    dve.tensor_reduce(osum[:, t], acc[:, t, 0:HPG * VH].rearrange("p (h a f) -> p h f a", a=VP, f=VF),
                                      AX_X, ALU.add).then_inc(acc_read, 1)

                def normalise(i, u, c):
                    n = NC * (UNITS * i + u) + c
                    dve.wait_ge(acc_read, TQ * (n + 1))
                    dve.reciprocal(rden[:, :, :], osum[:, :, :, HD]).then_inc(rden_done, 1)
                    dve.wait_ge(rden_done, n + 1)
                    dve.tensor_tensor(o[:, c % 2].rearrange("p t (h f) -> p t h f", f=HD), osum[:, :, :, 0:HD],
                                      rden[:, :, :].unsqueeze(3).to_broadcast([P, TQ, HPG, HD]), ALU.mult
                                      ).then_inc(o_done, 1)

                def turned(i, u, c, at, before, bank):
                    cols = slice(c * QC, (c + 1) * QC)
                    dve.wait_ge(work_done, before + at + 1)
                    dve.tensor_copy(oT[:, 0, u % UNITS, cols], pw[:, bank, 0:QC]).then_inc(oT_hi, 1)
                    dve.wait_ge(oT_hi, NC * (UNITS * i + u) + c + 1)
                    dve.tensor_tensor(oT[:, 1, u % UNITS, cols], pw[:, bank, 0:QC],
                                      oT[:, 0, u % UNITS, cols].bitcast(F32), ALU.subtract).then_inc(released, 1)

                def wo_stats(i, m, at, before, bank):
                    t, part = m // 2, m % 2
                    s, n = t % YR, QT * i + t
                    dve.wait_ge(work_done, before + at + 1)
                    dve.bn_stats(stats[:, s, part, :], pw[:, bank, 0:DH]).then_inc(stats_done, 1)
                    if part == 0:
                        wait(dve, y_stored[s], 16 * (QT // YR * i + t // YR))
                    dve.tensor_copy(y[:, s, part * DH:(part + 1) * DH], pw[:, bank, 0:DH]).then_inc(released, 1)
                    if part == 1:
                        dve.wait_ge(stats_done, 2 * n + 2)
                        dve.tensor_copy(seen[:, :], stats[:, s, 0, 0:1])
                        dve.bn_aggr(mv[:, s, :], stats[:, s, :, :]).then_inc(mv_done, 1)

                def shared(i, at, before, what, unit, m, stage):
                    bank = ((before if isinstance(before, int) else work_before(0, stage)) + at) % 2
                    if what == "turn":
                        turned(i, unit, m, at, before, bank)
                    elif what == "wo":
                        wo_stats(i + unit, m, at, before, bank)
                    else:
                        maxima(i, at, before, what, unit, m, bank)

                def run(i, stage):
                    before = work_before(i, stage)
                    for u, k in stage.slots:
                        for at, what, unit, m in stage.at(u, k):
                            shared(i, at, before, what, unit, m, stage)
                        e = stage.earlier(u, k, LAG)
                        if e:
                            c, j = STEPS[e[1]]
                            if j >= TQ * c:
                                sums(i, e[0], c, j - TQ * c)
                            if e[1] in LAST_OF_C:
                                normalise(i, e[0], c)

                for at, (what, m) in enumerate(AHEAD):
                    shared(0, at, 0, what, 0, m, None)
                run_all(dve, run)

            @block.gpsimd
            def _(pool):
                def low(i, u, k):
                    v, off = UNITS * i + u, first_query(k)
                    pool.wait_ge(hi_done, NS * v + k + 1)
                    pool.tensor_tensor(prob_lo[:, k % HR, :, off:QC], prob[:, k % PR, :, off:QC],
                                       prob_hi[:, k % HR, :, off:QC], ALU.subtract).then_inc(lo_done, 1)

                def wo_small(i, t):
                    n, s = QT * i + t, t % YR
                    pool.wait_ge(mv_done, n + 1)
                    c = 4 * n
                    pool.tensor_tensor(small[:, s, 0:1], mv[:, s, 1:2], eps[:, :], ALU.add).then_inc(small_done, 1)
                    pool.wait_ge(small_done, c + 1)
                    pool.tensor_tensor(small[:, s, 1:2], small[:, s, 0:1], half[:, :], ALU.pow).then_inc(small_done, 1)
                    pool.wait_ge(small_done, c + 2)
                    pool.tensor_tensor(small[:, s, 2:3], mv[:, s, 0:1], small[:, s, 1:2], ALU.mult
                                       ).then_inc(small_done, 1)
                    pool.wait_ge(small_done, c + 3)
                    pool.tensor_tensor(small[:, s, 3:4], small[:, s, 2:3], minus[:, :], ALU.mult
                                       ).then_inc(small_done, 1)

                def wo_add(i, t):
                    n, s = QT * i + t, t % YR
                    pool.wait_ge(y_norm, n + 1)
                    pool.wait_ge(xr_loaded[t % 2], 16 * (QT // 2 * i + t // 2 + 1))
                    pool.tensor_tensor(y[:, s, :], y[:, s, :], xr[:, t % 2, :], ALU.add).then_inc(y_done, 1)

                def run(i, stage):
                    for u, k in stage.slots:
                        e = stage.earlier(u, k, 1)
                        if e:
                            low(i, *e)
                        for b, t in stage.tiles(u, k, WO_SMALL):
                            wo_small(i + b, t)
                        for b, t in stage.tiles(u, k, WO_ADD):
                            wo_add(i + b, t)

                run_all(pool, run)


def ffn_phase(nc, x1, w1, b1, phases, w_real, w_imag, w2, b2, out):
    TWO_PI = 2 * math.pi
    TURN = 6.283185
    PI_IN = 3.1415925
    SLOPE = 0.1
    ROUND = 1.5 * 2 ** 23
    C1 = 201 / 32
    C2 = round((TWO_PI - C1) * 2 ** 20) / 2 ** 20
    C3 = TWO_PI - C1 - C2
    NF = FF // P
    HB = 3
    AR = 2
    STATS_AT, APPLY_AT = 6, 8
    TR_AT = {10: 0, 11: 1, 12: 2, 13: 3}
    POST_AT = (2, 4)

    ctx = ExitStack()
    with ctx:
        def sb(name, shape, dt=F32):
            return ctx.enter_context(nc.sbuf_tensor("f_" + name, shape, dt))

        def sem(name):
            return ctx.enter_context(nc.semaphore("f_" + name))

        w1s = sb("w1", [P, 2, KT, FF], F32R)
        w2s = sb("w2", [P, 2, NF, D], F32R)
        xT = sb("xT", [P, 2, 2, KT, CH], F32R)
        xin = sb("x", [P, 2, TPC, D])
        work = sb("work", [P, TPC, D])
        act_r = sb("act", [P, AR, 2, CH], F32R)
        hidden_work = sb("hidden_work", [P, 4, CH])
        arg = hidden_work[:, 0:2]
        whole = hidden_work[:, 2:4]
        b2s = sb("b2", [P, D])
        ident = sb("ident", [P, P])
        vec_rows = sb("vec_rows", [4 * NF, P])
        vec = sb("vec", [P, 4, NF])
        tmp = sb("tmp", [P, 12, NF])
        coef = sb("coef", [P, NF])
        turn0 = sb("turn0", [P, NF])
        stats = sb("stats", [P, 2, TPC, 6])
        seen = sb("seen", [P, 1])
        mv = sb("mv", [P, 2, TPC, 2])
        ve = sb("ve", [P, 2, TPC])
        rstd = sb("rstd", [P, 2, TPC])
        half = sb("half", [P, TPC])
        eps = sb("eps", [P, TPC])
        ph = ctx.enter_context(nc.psum_tensor("f_ph", [P, HB, CH], F32))
        pt = ctx.enter_context(nc.psum_tensor("f_pt", [P, CH], F32))
        py = ctx.enter_context(nc.psum_tensor("f_py", [P, TPC, D], F32))

        w_loaded = [sem(f"w_loaded{n}") for n in range(3)]
        w_hi, w_lo = sem("w_hi"), sem("w_lo")
        const, vec_loaded, b2_loaded = sem("const"), sem("vec_loaded"), sem("b2_loaded")
        vec_turned, vec_step, trig = sem("vec_turned"), sem("vec_step"), sem("trig")
        x_loaded = [sem(f"x_loaded{e}") for e in range(2)]
        stats_done, mv_done, ve_done, rstd_done = sem("stats_done"), sem("mv_done"), sem("ve_done"), sem("rstd_done")
        normed, tr_done, tr_hi, tr_lo = sem("normed"), sem("tr_done"), sem("tr_hi"), sem("tr_lo")
        h_done, arg_done, whole_done, frac_done = sem("h_done"), sem("arg_done"), sem("whole_done"), sem("frac_done")
        sin_done, q_done, relu_done, act_hi, act_lo = (sem(n) for n in ("sin_done", "q_done", "relu_done", "act_hi",
                                                                        "act_lo"))
        w2_used, w2_done, y_read, y_normed, y_final, y_stored = (sem(n) for n in ("w2_used", "w2_done", "y_read", "y_normed", "y_final",
                                                                         "y_stored"))
        x1_v = x1[2:BATCH + 2].rearrange("b (c t p) d -> (b c) p t d", p=P, t=TPC)
        out_v = out.rearrange("b (c t p) d -> (b c) p t d", p=P, t=TPC)
        raw = [a.rearrange("p t d -> p (t d)") for a in (xin[:, 1], work[:, :, :], hidden_work[:, :, :])]
        b2_rows = b2.rearrange("(o d) -> o d", o=1).broadcast_to([P, D])

        with nc.Block() as wblock:
            pieces = [(w1[k * P:(k + 1) * P, :], (lambda part, k=k: w1s[:, part, k, :])) for k in range(KT)]
            pieces += [(w2.rearrange("(g k p) d -> g p k d", k=4, p=P)[g],
                        (lambda part, g=g: w2s[:, part, 4 * g:4 * g + 4, :].rearrange("p k d -> p (k d)")))
                       for g in range(NF // 4)]
            def small_vectors(sp):
                for n, v in enumerate((b1, phases, w_real, w_imag)):
                    sp.dma_start(vec_rows[n * NF:(n + 1) * NF, :], v.rearrange("(f p) -> f p", p=P)
                                 ).then_inc(vec_loaded, 16)

            def first_chunk(sp):
                sp.dma_start(xin[:, 0], x1_v[0]).then_inc(x_loaded[0], 16)
                sp.dma_start(b2s[:, :], b2_rows).then_inc(b2_loaded, 16)

            def vectors(dve):
                steps = [0]

                def then(ins):
                    steps[0] += 1
                    ins.then_inc(vec_step, 1)
                    dve.wait_ge(vec_step, steps[0])

                bias, th, wr, wi = (vec[:, n, :] for n in range(4))
                turns, thr, sin_a, cos_a, over, sin_t, cos_t = (tmp[:, n, :] for n in range(7))
                dve.wait_ge(vec_turned, 1)
                then(dve.tensor_copy(vec[:, :, :].rearrange("p v f -> p (v f)"), pt[:, 0:4 * NF]))
                then(dve.tensor_scalar(turns, th, 1 / TWO_PI, ROUND, ALU.mult, ALU.add))
                then(dve.tensor_scalar(turns, turns, -ROUND, None, ALU.add))
                then(dve.scalar_tensor_tensor(thr, turns, -C1, th, ALU.mult, ALU.add))
                then(dve.scalar_tensor_tensor(thr, turns, -C2, thr, ALU.mult, ALU.add))
                then(dve.scalar_tensor_tensor(thr, turns, -C3, thr, ALU.mult, ALU.add))
                then(dve.tensor_scalar(sin_a, thr, PI_IN, -PI_IN, ALU.min, ALU.max))
                then(dve.tensor_scalar(cos_a, thr, math.pi / 2, None, ALU.add))
                then(dve.tensor_scalar(over, cos_a, PI_IN, -TWO_PI, ALU.is_gt, ALU.mult))
                then(dve.tensor_tensor(cos_a, cos_a, over, ALU.add))
                then(dve.tensor_scalar(cos_a, cos_a, PI_IN, -PI_IN, ALU.min, ALU.max))
                then(dve.scalar_tensor_tensor(turn0[:, :], bias, SLOPE, thr, ALU.mult, ALU.add))
                then(dve.tensor_scalar(turn0[:, :], turn0[:, :], 1 / TWO_PI, None, ALU.mult))

            def sines(act):
                act.wait_ge(vec_step, 11)
                act.activation(tmp[:, 5, :], tmp[:, 2, :], ACT.Sin).then_inc(trig, 1)
                act.activation(tmp[:, 6, :], tmp[:, 3, :], ACT.Sin).then_inc(trig, 1)

            split_weights(wblock, pieces, raw, w_loaded, w_hi, w_lo, first_chunk, small_vectors,
                          sines, vectors)

            @wblock.tensor
            def _(pe):
                pe.wait_ge(vec_loaded, 64)
                pe.wait_ge(const, 2)
                pe.transpose(pt[:, 0:4 * NF], vec_rows[:, :], ident[0:4 * NF, 0:4 * NF]).then_inc(vec_turned, 1)

            @wblock.gpsimd
            def _(pool):
                identity_matrix(pool, ident[:, :], const)
                pool.memset(half[:, :], -0.5)
                pool.memset(eps[:, :], EPS)

        with nc.Block() as block:
            @block.sync
            def _(sp):
                def load(n, e):
                    sp.dma_start(xin[:, e], x1_v[n]).then_inc(x_loaded[e], 16)

                def finish(n):
                    sp.wait_ge(y_final, n + 1)
                    sp.dma_start(out_v[n], work[:, :, :]).then_inc(y_stored, 16)

                sp.sem_inc(y_stored, START)
                load(1, 1)
                with sp.Fori(0, BATCH - 1) as i:
                    for e in range(2):
                        finish(2 * i + e)
                        load(2 * i + e + 2, e)
                for e in range(2):
                    finish(2 * (BATCH - 1) + e)
                sp.wait_ge(y_stored, 16 * NCH + START)

            @block.gpsimd
            def _(pool):
                def rstd_of(number, which):
                    pool.wait_ge(mv_done, number + 1)
                    pool.tensor_tensor(ve[:, which], mv[:, which, :, 1], eps[:, :], ALU.add).then_inc(ve_done, 1)
                    pool.wait_ge(ve_done, number + 1)
                    pool.tensor_tensor(rstd[:, which], ve[:, which], half[:, :], ALU.pow).then_inc(rstd_done, 1)

                rstd_of(0, 1)
                rstd_of(1, 1)
                with pool.Fori(1, NCH - 1) as n:
                    rstd_of(2 * n, 0)
                    rstd_of(2 * n + 1, 1)
                rstd_of(2 * NCH - 2, 0)
                rstd_of(2 * NCH - 1, 0)

            @block.vector
            def _(dve):
                def statistics(number, which, src):
                    for t in range(TPC):
                        last = dve.bn_stats(stats[:, which, t, :], src[:, t, :])
                    last.then_inc(stats_done, 1)
                    dve.wait_ge(stats_done, number + 1)
                    dve.tensor_copy(seen[:, :], stats[:, which, 0, 0:1])
                    for t in range(TPC):
                        last = dve.bn_aggr(mv[:, which, t, :], stats[:, which, t, :])
                    last.then_inc(mv_done, 1)

                def scale(number, which, dst, src, done):
                    dve.wait_ge(rstd_done, number + 1)
                    for t in range(TPC):
                        last = dve.tensor_scalar(dst[:, t, :], src[:, t, :], mv[:, which, t, 0:1],
                                                 rstd[:, which, t:t + 1], ALU.subtract, ALU.mult)
                    last.then_inc(done, 1)

                def transposed_lo(n, e, k):
                    dve.wait_ge(tr_hi, KT * n + k + 1)
                    dve.tensor_tensor(xT[:, e, 1, k, :], pt[:, :], xT[:, e, 0, k, :].bitcast(F32), ALU.subtract
                                      ).then_inc(tr_lo, 1)

                def post_stats(n, number):
                    dve.wait_ge(y_read, TPC * n + TPC + START)
                    statistics(number, 0, work)

                def post_residual(n, e, number):
                    scale(number, 0, work, work, y_normed)
                    dve.wait_ge(y_normed, n + 1)
                    dve.tensor_tensor(work[:, :, :], work[:, :, :], xin[:, e], ALU.add).then_inc(y_final, 1)

                def chunk(i, e, first, last):
                    n = 2 * i + e
                    number = 2 * n
                    for f in range(NF + 1):
                        F = NF * n + f
                        s = f % 2
                        if f < NF:
                            dve.wait_ge(arg_done, F + 1)
                            dve.tensor_scalar(whole[:, s, :], arg[:, s, :], ROUND, -ROUND, ALU.add, ALU.add
                                              ).then_inc(whole_done, 1)
                            dve.wait_ge(whole_done, F + 1)
                            dve.tensor_tensor(whole[:, s, :], arg[:, s, :], whole[:, s, :], ALU.subtract
                                              ).then_inc(frac_done, 1)
                        if f >= 1:
                            r = (f - 1) % AR
                            dve.wait_ge(act_hi, F)
                            dve.tensor_tensor(act_r[:, r, 1, :], arg[:, 1 - s, :], act_r[:, r, 0, :].bitcast(F32),
                                              ALU.subtract).then_inc(act_lo, 1)
                        if f < NF:
                            dve.wait_ge(sin_done, F + 1)
                            dve.scalar_tensor_tensor(whole[:, s, :], arg[:, s, :], coef[:, f:f + 1], ph[:, f % HB, :],
                                                     ALU.mult, ALU.add).then_inc(q_done, 1)
                        if f == POST_AT[0] and not first:
                            post_stats(n - 1, number)
                        if f == POST_AT[1] and not first:
                            post_residual(n - 1, 1 - e, number)
                        if f == STATS_AT and not last:
                            dve.wait_ge(x_loaded[1 - e], 16 * (i + 1 + e))
                            statistics(number + 1, 1, xin[:, 1 - e])
                        if f == APPLY_AT and not last:
                            if not first:
                                dve.wait_ge(y_stored, 16 * n + START)
                            scale(number + 1, 1, work, xin[:, 1 - e], normed)
                        if f in TR_AT and not last:
                            transposed_lo(n + 1, 1 - e, TR_AT[f])
                    if not last:
                        dve.wait_ge(tr_done, KT * (n + 2))
                    else:
                        dve.wait_ge(y_stored, 16 * n + START)
                    for t in range(TPC):
                        dve.wait_ge(w2_done, TPC * n + t + 1 + START)
                        dve.tensor_tensor(work[:, t, :], py[:, t, :], b2s[:, :], ALU.add).then_inc(y_read, 1)

                for s in (q_done, y_read, act_lo):
                    dve.sem_inc(s, START)
                steps = [13]

                def then(ins):
                    steps[0] += 1
                    ins.then_inc(vec_step, 1)
                    dve.wait_ge(vec_step, steps[0])

                wr, wi, sin_t, cos_t = vec[:, 2, :], vec[:, 3, :], tmp[:, 5, :], tmp[:, 6, :]
                dve.wait_ge(trig, 2)
                then(dve.tensor_tensor(cos_t, cos_t, wr, ALU.mult))
                then(dve.tensor_tensor(sin_t, sin_t, wi, ALU.mult))
                then(dve.tensor_tensor(cos_t, cos_t, sin_t, ALU.add))
                then(dve.tensor_tensor(cos_t, cos_t, wi, ALU.mult))
                then(dve.tensor_scalar(coef[:, :], cos_t, SLOPE, None, ALU.mult))
                dve.wait_ge(x_loaded[0], 16)
                dve.wait_ge(b2_loaded, 16)
                statistics(0, 1, xin[:, 0])
                scale(0, 1, work, xin[:, 0], normed)
                for k in range(KT):
                    transposed_lo(0, 0, k)
                chunk(0, 0, True, False)
                chunk(0, 1, False, False)
                with dve.Fori(1, BATCH - 1) as i:
                    for e in range(2):
                        chunk(i, e, False, False)
                for e in range(2):
                    chunk(BATCH - 1, e, False, e == 1)
                post_stats(NCH - 1, 2 * NCH - 1)
                post_residual(NCH - 1, 1, 2 * NCH - 1)

            @block.scalar
            def _(act):
                def transposed_hi(n, e, k):
                    act.wait_ge(tr_done, KT * n + k + 1)
                    act.activation(xT[:, e, 0, k, :], pt[:, :], ACT.Copy).then_inc(tr_hi, 1)

                def chunk(i, e, last):
                    n = 2 * i + e
                    for f in range(NF + 1):
                        F = NF * n + f
                        s = f % 2
                        if f < NF:
                            act.wait_ge(h_done, F + 1)
                            act.wait_ge(act_lo, NF * n + max(f - 1, 0) + START)
                            act.activation(arg[:, s, :], ph[:, f % HB, :], ACT.Identity, bias=turn0[:, f:f + 1],
                                           scale=SLOPE / TWO_PI).then_inc(arg_done, 1)
                        if f >= 1:
                            r = (f - 1) % AR
                            act.wait_ge(q_done, F + START)
                            act.activation(arg[:, 1 - s, :], whole[:, 1 - s, :], ACT.Relu,
                                           bias=vec[:, 0, f - 1:f]).then_inc(relu_done, 1)
                            if f - 1 >= AR:
                                act.wait_ge(w2_used, (NF - 1) * n + f - AR)
                            else:
                                act.wait_ge(w2_done, TPC * n + START)
                            act.wait_ge(relu_done, F)
                            act.activation(act_r[:, r, 0, :], arg[:, 1 - s, :], ACT.Copy).then_inc(act_hi, 1)
                        if f < NF:
                            act.wait_ge(frac_done, F + 1)
                            act.activation(arg[:, s, :], whole[:, s, :], ACT.Sin, scale=TURN).then_inc(sin_done, 1)
                        if f in TR_AT and not last:
                            transposed_hi(n + 1, 1 - e, TR_AT[f])

                for k in range(KT):
                    transposed_hi(0, 0, k)
                with act.Fori(0, BATCH - 1) as i:
                    for e in range(2):
                        chunk(i, e, False)
                for e in range(2):
                    chunk(BATCH - 1, e, e == 1)

            @block.tensor
            def _(pe):
                def transposes(n, e, k, first=False):
                    if not (first and k == 0):
                        pe.wait_ge(tr_lo, KT * n + k)
                    if k == 0:
                        pe.wait_ge(normed, n + 1)
                    for t in range(TPC):
                        last = pe.transpose(pt[:, t * P:(t + 1) * P], work[:, t, k * P:(k + 1) * P], ident[:, :])
                    last.then_inc(tr_done, 1)

                def hidden(n, e, f):
                    pe.wait_ge(q_done, NF * n + (f - HB + 1 if f >= HB else 0) + START)
                    if f == 0:
                        pe.wait_ge(tr_lo, KT * n + KT)
                    terms = [(k, a, b) for k in range(KT) for a, b in PASSES]
                    for j, (k, a, b) in enumerate(terms):
                        last = pe.matmul(ph[:, f % HB, :], w1s[:, a, k, f * P:(f + 1) * P], xT[:, e, b, k, :],
                                         start=(j == 0), stop=(j == len(terms) - 1))
                    last.then_inc(h_done, 1)

                def output(n, f):
                    pe.wait_ge(act_lo, NF * n + f + 1 + START)
                    if f == 0:
                        pe.wait_ge(y_read, TPC * n + START)
                    for t in range(TPC):
                        for j, (a, b) in enumerate(PASSES):
                            last = pe.matmul(py[:, t, :], act_r[:, f % AR, b, t * P:(t + 1) * P], w2s[:, a, f, :],
                                             start=(f == 0 and j == 0), stop=(f == NF - 1 and j == len(PASSES) - 1))
                        if f == NF - 1:
                            last.then_inc(w2_done, 1)
                    if f < NF - 1:
                        last.then_inc(w2_used, 1)

                def chunk(i, e, last):
                    n = 2 * i + e
                    for f in range(NF + 2):
                        if f < NF:
                            hidden(n, e, f)
                        if f in TR_AT and not last:
                            transposes(n + 1, 1 - e, TR_AT[f])
                        if f >= 2:
                            output(n, f - 2)

                pe.sem_inc(w2_done, START)
                for k in range(KT):
                    transposes(0, 0, k, first=True)
                with pe.Fori(0, BATCH - 1) as i:
                    for e in range(2):
                        chunk(i, e, False)
                for e in range(2):
                    chunk(BATCH - 1, e, e == 1)


def layer(nc, x, w_qvk, w_o, w1, b1, phases, w_real, w_imag, w2, b2, out):
    qk_parts = nc.dram_tensor("qk_parts", [BATCH, 2 * GROUPS, 2, P, SEQ], F32, kind="Internal").ap()
    v_parts = nc.dram_tensor("v_parts", [BATCH, SEQ, VROW], BF16, kind="Internal").ap()
    x1 = nc.dram_tensor("x1", [BATCH + 2, SEQ, D], F32, kind="Internal").ap()
    qkv_phase(nc, x, w_qvk, qk_parts, v_parts)
    attention_phase(nc, x, w_o, qk_parts, v_parts, x1)
    ffn_phase(nc, x1, w1, b1, phases, w_real, w_imag, w2, b2, out)


_INS = ["L0_attn_h", "L0_attn_Wqvk", "L0_attn_Wo", "L0_ffn_W1", "L0_ffn_b1", "L0_ffn_quantum_phases",
        "L0_ffn_quantum_weights_real", "L0_ffn_quantum_weights_imag", "L0_ffn_W2", "L0_ffn_b2"]
_OUTS = [((BATCH, SEQ, D), "float32")]


def kernel(**inputs):
    import numpy as _np
    import concourse.bacc as _bacc
    from concourse import mybir as _mybir
    from concourse.bass_utils import run_bass_kernel_spmd as _run

    nc = _bacc.Bacc("TRN2", target_bir_lowering=False, num_devices=1)
    arrays, args = {}, []
    for name in _INS:
        a = _np.ascontiguousarray(inputs[name])
        arrays[f"in_{name}_dram"] = a
        args.append(nc.dram_tensor(f"in_{name}_dram", a.shape, _mybir.dt.from_np(a.dtype), kind="ExternalInput").ap())
    for i, (shape, dtype) in enumerate(_OUTS):
        dt = _mybir.dt.from_np(_np.dtype(dtype))
        args.append(nc.dram_tensor(f"out_{i}_dram", shape, dt, kind="ExternalOutput").ap())
    layer(nc, *args)
    r = _run(nc, [arrays], core_ids=[0])
    got = tuple(r.results[0][f"out_{i}_dram"] for i in range(len(_OUTS)))
    return got[0]
```
